# Optimizing a Trainium2 kernel written in Bass

```python
import numpy as np
import jax
import jax.numpy as jnp

def _softmax(x, axis=-1):
    return jax.nn.softmax(x, axis=axis)

def _gelu(x):
    return jax.nn.gelu(x, approximate=True)

def _silu(x):
    return jax.nn.silu(x)

def _sigmoid(x):
    return jax.nn.sigmoid(x)

def _layernorm(x, axis=-1, eps=1e-05):
    m = jnp.mean(x, axis=axis, keepdims=True)
    v = jnp.var(x, axis=axis, keepdims=True)
    return (x - m) / jnp.sqrt(v + eps)

def _scatter_add(tgt, idx, src, axis=0):
    return tgt.at[idx].add(src)

def _segment_sum(src, seg, n):
    return jax.ops.segment_sum(src, seg, n)
kernel_name = 'mk_macaron_d2_jaxref_r4_a55e92'

def setup_inputs(seed: int=0):
    np.random.seed(seed)
    _w = jnp.asarray

    def _L0_attn_setup():
        import jax, jax.numpy as jnp
        import numpy as np
        D = 256
        H = 16
        DK = D // H
        CHUNK = 64
        EPS = 1e-05

        def _layernorm_noaffine(k):
            mu = jnp.mean(k, axis=-1, keepdims=True)
            var = jnp.mean((k - mu) ** 2, axis=-1, keepdims=True)
            return (k - mu) / jnp.sqrt(var + EPS)

        def _linear_attn(x, W_qkv, W_o):
            B, L, Dm = x.shape
            qkv = (x @ W_qkv).reshape(B, L, 3, H, DK)
            q, k, v = (qkv[:, :, 0], qkv[:, :, 1], qkv[:, :, 2])
            k = _layernorm_noaffine(k)
            nC = L // CHUNK
            to_chunks = lambda t: t.reshape(B, nC, CHUNK, H, DK).transpose(1, 0, 2, 3, 4)
            qc, kc, vc = (to_chunks(q), to_chunks(k), to_chunks(v))
            causal = jnp.tril(jnp.ones((CHUNK, CHUNK), dtype=bool))

            def step(S, chunk):
                q_c, k_c, v_c = chunk
                inter = jnp.einsum('bhde,bthe->bthd', S, q_c)
                scores = jnp.einsum('bthd,bshd->bhts', q_c, k_c)
                scores = jnp.where(causal, scores, 0.0)
                intra = jnp.einsum('bhts,bshd->bthd', scores, v_c)
                S = S + jnp.einsum('bthd,bthe->bhde', v_c, k_c)
                return (S, inter + intra)
            S0 = jnp.zeros((B, H, DK, DK), dtype=x.dtype)
            _, ys = jax.lax.scan(step, S0, (qc, kc, vc))
            y = ys.transpose(1, 0, 2, 3, 4).reshape(B, L, Dm)
            return y @ W_o
        key = jax.random.key(seed)
        k1, k2, k3 = jax.random.split(key, 3)
        x = jax.random.normal(k1, (4, 1024, D), dtype=jnp.float32)
        W_qkv = jax.random.normal(k2, (D, 3 * D), dtype=jnp.float32) * 0.02
        W_o = jax.random.normal(k3, (D, D), dtype=jnp.float32) * 0.02
        return {'x': x, 'W_qkv': W_qkv, 'W_o': W_o}
    _L0_attn_in = _L0_attn_setup()

    def _L0_ffn_setup():
        import jax, jax.numpy as jnp
        import numpy as np
        DIM = 256

        def _reference_tuple_inner(x, W_r, W_k, W_v, mu_r, mu_k):
            B, T, C = x.shape
            x_prev = jnp.concatenate([jnp.zeros((B, 1, C), x.dtype), x[:, :-1, :]], axis=1)
            xr = mu_r * x + (1.0 - mu_r) * x_prev
            xk = mu_k * x + (1.0 - mu_k) * x_prev
            r = jax.nn.sigmoid(jnp.einsum('btc,dc->btd', xr, W_r))
            k = jnp.einsum('btc,dc->btd', xk, W_k)
            k_act = jnp.square(jax.nn.relu(k))
            out = r * jnp.einsum('btc,dc->btd', k_act, W_v)
            new_state = x[:, -1, :]
            return (out, new_state)
        key = jax.random.key(seed)
        ks = jax.random.split(key, 6)
        B, T, C = (8, 512, DIM)
        x = jax.random.normal(ks[0], (B, T, C), dtype=jnp.float32)
        s = 1.0 / np.sqrt(C)
        W_r = jax.random.uniform(ks[1], (C, C), jnp.float32, -s, s)
        W_k = jax.random.uniform(ks[2], (C, C), jnp.float32, -s, s)
        W_v = jax.random.uniform(ks[3], (C, C), jnp.float32, -s, s)
        mu_r = jax.random.uniform(ks[4], (C,), jnp.float32)
        mu_k = jax.random.uniform(ks[5], (C,), jnp.float32)
        return {'x': x, 'W_r': W_r, 'W_k': W_k, 'W_v': W_v, 'mu_r': mu_r, 'mu_k': mu_k}
    _L0_ffn_in = _L0_ffn_setup()

    def _L1_attn_setup():
        import jax, jax.numpy as jnp
        import numpy as np
        EMB = 256
        HEADS = 16
        HEAD_DIM = EMB // HEADS
        ROPE_BASE = 10000.0

        def rotate_half(x):
            x1 = x[..., ::2]
            x2 = x[..., 1::2]
            return jnp.stack((-x2, x1), axis=-1).reshape(x.shape)

        def rope_cos_sin(seq_len, head_dim):
            inv_freq = 1.0 / ROPE_BASE ** (jnp.arange(0, head_dim, 2, dtype=jnp.float32) / head_dim)
            pos = jnp.arange(seq_len, dtype=jnp.float32)
            freqs = jnp.outer(pos, inv_freq)
            emb = jnp.concatenate([freqs, freqs], -1)
            return (jnp.cos(emb)[None, None], jnp.sin(emb)[None, None])
        key = jax.random.key(seed)
        ks = jax.random.split(key, 5)
        B, S = (2, 512)
        x = jax.random.normal(ks[0], (B, S, EMB), dtype=jnp.float32)
        scale = EMB ** (-0.5)
        Wq = jax.random.normal(ks[1], (EMB, EMB), dtype=jnp.float32) * scale
        Wk = jax.random.normal(ks[2], (EMB, EMB), dtype=jnp.float32) * scale
        Wv = jax.random.normal(ks[3], (EMB, EMB), dtype=jnp.float32) * scale
        Wo = jax.random.normal(ks[4], (EMB, EMB), dtype=jnp.float32) * scale
        return {'x': x, 'Wq': Wq, 'Wk': Wk, 'Wv': Wv, 'Wo': Wo}
    _L1_attn_in = _L1_attn_setup()

    def _L1_ffn_setup():
        import jax, jax.numpy as jnp
        import numpy as np
        B, C, D, O = (4, 1024, 256, 256)
        PROJ = 64
        RANKS = [1, 2, 4, 8]
        E = len(RANKS)
        CLAMP_MAX = float(np.log(1.0 / 0.01))

        def _l2norm(v, axis):
            return v / jnp.maximum(jnp.linalg.norm(v, axis=axis, keepdims=True), 1e-12)
        key = jax.random.key(seed)
        ks = jax.random.split(key, 16)
        inp = {'x': jax.random.normal(ks[0], (B, C, D), dtype=jnp.float32), 'W': jax.random.normal(ks[1], (O, D), dtype=jnp.float32) / np.sqrt(D), 'Wp': jax.random.normal(ks[2], (PROJ, D), dtype=jnp.float32) / np.sqrt(D), 'bp': jnp.zeros((PROJ,), dtype=jnp.float32), 'sim': jax.random.normal(ks[3], (PROJ, E), dtype=jnp.float32) * 0.01, 'temp': jnp.full((1,), np.log(1.0 / 0.5), dtype=jnp.float32)}
        for i, r in enumerate(RANKS):
            inp[f'Wd{i}'] = jax.random.normal(ks[4 + 2 * i], (r, D), dtype=jnp.float32) / r
            inp[f'Wu{i}'] = jax.random.normal(ks[5 + 2 * i], (O, r), dtype=jnp.float32) * 0.01
        return inp
    _L1_ffn_in = _L1_ffn_setup()
    _d = {'L0_attn_x': _L0_attn_in['x'], 'L0_attn_W_qkv': _L0_attn_in['W_qkv'], 'L0_attn_W_o': _L0_attn_in['W_o'], 'L0_ffn_W_r': _L0_ffn_in['W_r'], 'L0_ffn_W_k': _L0_ffn_in['W_k'], 'L0_ffn_W_v': _L0_ffn_in['W_v'], 'L0_ffn_mu_r': _L0_ffn_in['mu_r'], 'L0_ffn_mu_k': _L0_ffn_in['mu_k'], 'L1_attn_Wq': _L1_attn_in['Wq'], 'L1_attn_Wk': _L1_attn_in['Wk'], 'L1_attn_Wv': _L1_attn_in['Wv'], 'L1_attn_Wo': _L1_attn_in['Wo'], 'L1_ffn_W': _L1_ffn_in['W'], 'L1_ffn_Wp': _L1_ffn_in['Wp'], 'L1_ffn_bp': _L1_ffn_in['bp'], 'L1_ffn_sim': _L1_ffn_in['sim'], 'L1_ffn_temp': _L1_ffn_in['temp'], 'L1_ffn_Wd0': _L1_ffn_in['Wd0'], 'L1_ffn_Wu0': _L1_ffn_in['Wu0'], 'L1_ffn_Wd1': _L1_ffn_in['Wd1'], 'L1_ffn_Wu1': _L1_ffn_in['Wu1'], 'L1_ffn_Wd2': _L1_ffn_in['Wd2'], 'L1_ffn_Wu2': _L1_ffn_in['Wu2'], 'L1_ffn_Wd3': _L1_ffn_in['Wd3'], 'L1_ffn_Wu3': _L1_ffn_in['Wu3']}
    _x0 = _d['L0_attn_x']
    _d['L0_attn_x'] = jax.random.normal(jax.random.fold_in(jax.random.key(seed), 1), (8, 1024, 256), dtype=_x0.dtype)
    del _x0
    return _d

def reference(L0_attn_x, L0_attn_W_qkv, L0_attn_W_o, L0_ffn_W_r, L0_ffn_W_k, L0_ffn_W_v, L0_ffn_mu_r, L0_ffn_mu_k, L1_attn_Wq, L1_attn_Wk, L1_attn_Wv, L1_attn_Wo, L1_ffn_W, L1_ffn_Wp, L1_ffn_bp, L1_ffn_sim, L1_ffn_temp, L1_ffn_Wd0, L1_ffn_Wu0, L1_ffn_Wd1, L1_ffn_Wu1, L1_ffn_Wd2, L1_ffn_Wu2, L1_ffn_Wd3, L1_ffn_Wu3):

    def _L0_attn_ref(x, W_qkv, W_o):
        import jax, jax.numpy as jnp
        import numpy as np
        D = 256
        H = 16
        DK = D // H
        CHUNK = 64
        EPS = 1e-05

        def _layernorm_noaffine(k):
            mu = jnp.mean(k, axis=-1, keepdims=True)
            var = jnp.mean((k - mu) ** 2, axis=-1, keepdims=True)
            return (k - mu) / jnp.sqrt(var + EPS)

        def _linear_attn(x, W_qkv, W_o):
            B, L, Dm = x.shape
            qkv = (x @ W_qkv).reshape(B, L, 3, H, DK)
            q, k, v = (qkv[:, :, 0], qkv[:, :, 1], qkv[:, :, 2])
            k = _layernorm_noaffine(k)
            nC = L // CHUNK
            to_chunks = lambda t: t.reshape(B, nC, CHUNK, H, DK).transpose(1, 0, 2, 3, 4)
            qc, kc, vc = (to_chunks(q), to_chunks(k), to_chunks(v))
            causal = jnp.tril(jnp.ones((CHUNK, CHUNK), dtype=bool))

            def step(S, chunk):
                q_c, k_c, v_c = chunk
                inter = jnp.einsum('bhde,bthe->bthd', S, q_c)
                scores = jnp.einsum('bthd,bshd->bhts', q_c, k_c)
                scores = jnp.where(causal, scores, 0.0)
                intra = jnp.einsum('bhts,bshd->bthd', scores, v_c)
                S = S + jnp.einsum('bthd,bthe->bhde', v_c, k_c)
                return (S, inter + intra)
            S0 = jnp.zeros((B, H, DK, DK), dtype=x.dtype)
            _, ys = jax.lax.scan(step, S0, (qc, kc, vc))
            y = ys.transpose(1, 0, 2, 3, 4).reshape(B, L, Dm)
            return y @ W_o
        return _linear_attn(x, W_qkv, W_o)

    def _L0_ffn_ref(x, W_r, W_k, W_v, mu_r, mu_k):
        import jax, jax.numpy as jnp
        import numpy as np
        DIM = 256

        def _reference_tuple_inner(x, W_r, W_k, W_v, mu_r, mu_k):
            B, T, C = x.shape
            x_prev = jnp.concatenate([jnp.zeros((B, 1, C), x.dtype), x[:, :-1, :]], axis=1)
            xr = mu_r * x + (1.0 - mu_r) * x_prev
            xk = mu_k * x + (1.0 - mu_k) * x_prev
            r = jax.nn.sigmoid(jnp.einsum('btc,dc->btd', xr, W_r))
            k = jnp.einsum('btc,dc->btd', xk, W_k)
            k_act = jnp.square(jax.nn.relu(k))
            out = r * jnp.einsum('btc,dc->btd', k_act, W_v)
            new_state = x[:, -1, :]
            return (out, new_state)
        return _reference_tuple_inner(x, W_r, W_k, W_v, mu_r, mu_k)[0]

    def _L1_attn_ref(x, Wq, Wk, Wv, Wo):
        import jax, jax.numpy as jnp
        import numpy as np
        EMB = 256
        HEADS = 16
        HEAD_DIM = EMB // HEADS
        ROPE_BASE = 10000.0

        def rotate_half(x):
            x1 = x[..., ::2]
            x2 = x[..., 1::2]
            return jnp.stack((-x2, x1), axis=-1).reshape(x.shape)

        def rope_cos_sin(seq_len, head_dim):
            inv_freq = 1.0 / ROPE_BASE ** (jnp.arange(0, head_dim, 2, dtype=jnp.float32) / head_dim)
            pos = jnp.arange(seq_len, dtype=jnp.float32)
            freqs = jnp.outer(pos, inv_freq)
            emb = jnp.concatenate([freqs, freqs], -1)
            return (jnp.cos(emb)[None, None], jnp.sin(emb)[None, None])
        B, S, E = x.shape

        def shape_heads(t):
            return t.reshape(B, S, HEADS, HEAD_DIM).transpose(0, 2, 1, 3)
        q = shape_heads(x @ Wq.T)
        k = shape_heads(x @ Wk.T)
        v = shape_heads(x @ Wv.T)
        cos, sin = rope_cos_sin(S, HEAD_DIM)
        q = q * cos + rotate_half(q) * sin
        k = k * cos + rotate_half(k) * sin
        scale = HEAD_DIM ** (-0.5)
        scores = jnp.einsum('bhqd,bhkd->bhqk', q, k) * scale
        causal = jnp.triu(jnp.ones((S, S), dtype=bool), k=1)
        scores = jnp.where(causal, -jnp.inf, scores)
        attn = jax.nn.softmax(scores, axis=-1)
        out = jnp.einsum('bhqk,bhkd->bhqd', attn, v)
        out = out.transpose(0, 2, 1, 3).reshape(B, S, E)
        return out @ Wo.T

    def _L1_ffn_ref(x, W, Wp, bp, sim, temp, Wd0, Wu0, Wd1, Wu1, Wd2, Wu2, Wd3, Wu3):
        import jax, jax.numpy as jnp
        import numpy as np
        B, C, D, O = (4, 1024, 256, 256)
        PROJ = 64
        RANKS = [1, 2, 4, 8]
        E = len(RANKS)
        CLAMP_MAX = float(np.log(1.0 / 0.01))

        def _l2norm(v, axis):
            return v / jnp.maximum(jnp.linalg.norm(v, axis=axis, keepdims=True), 1e-12)
        base = jnp.einsum('bcd,od->bco', x, W)
        xf = x.reshape(-1, x.shape[-1])
        proj = _l2norm(xf @ Wp.T + bp, axis=1)
        simn = _l2norm(sim, axis=0)
        scale = jnp.exp(jnp.minimum(temp, CLAMP_MAX))
        logits = proj @ simn * scale
        lw = jax.nn.softmax(logits, axis=1)
        top1 = jnp.argmax(lw, axis=1)
        ret = jnp.where(jnp.arange(E)[None, :] == top1[:, None], lw, 0.0)
        ret = ret.reshape(x.shape[0], x.shape[1], E)
        downs = (Wd0, Wd1, Wd2, Wd3)
        ups = (Wu0, Wu1, Wu2, Wu3)
        l = jnp.stack([jnp.einsum('bcr,or->bco', jnp.einsum('bcd,rd->bcr', x, d), u) for d, u in zip(downs, ups)], axis=2)
        res = jnp.sum(ret[..., None] * l, axis=2)
        return base + res
    x = L0_attn_x
    x = x + 0.5 * _L0_ffn_ref(_layernorm(x, axis=-1), L0_ffn_W_r, L0_ffn_W_k, L0_ffn_W_v, L0_ffn_mu_r, L0_ffn_mu_k)
    x = x + _L0_attn_ref(_layernorm(x, axis=-1), L0_attn_W_qkv, L0_attn_W_o)
    x = x + 0.5 * _L0_ffn_ref(_layernorm(x, axis=-1), L0_ffn_W_r, L0_ffn_W_k, L0_ffn_W_v, L0_ffn_mu_r, L0_ffn_mu_k)
    x = x + 0.5 * _L1_ffn_ref(_layernorm(x, axis=-1), L1_ffn_W, L1_ffn_Wp, L1_ffn_bp, L1_ffn_sim, L1_ffn_temp, L1_ffn_Wd0, L1_ffn_Wu0, L1_ffn_Wd1, L1_ffn_Wu1, L1_ffn_Wd2, L1_ffn_Wu2, L1_ffn_Wd3, L1_ffn_Wu3)
    x = x + _L1_attn_ref(_layernorm(x, axis=-1), L1_attn_Wq, L1_attn_Wk, L1_attn_Wv, L1_attn_Wo)
    x = x + 0.5 * _L1_ffn_ref(_layernorm(x, axis=-1), L1_ffn_W, L1_ffn_Wp, L1_ffn_bp, L1_ffn_sim, L1_ffn_temp, L1_ffn_Wd0, L1_ffn_Wu0, L1_ffn_Wd1, L1_ffn_Wu1, L1_ffn_Wd2, L1_ffn_Wu2, L1_ffn_Wd3, L1_ffn_Wu3)
    return x

_drawn_inputs = setup_inputs


def setup_inputs(seed=0):
    import zlib

    import numpy as np

    out = dict(_drawn_inputs(seed))
    spreads = {'L1_ffn_bp': (0.0, 0.8)}
    factors = {'L0_ffn_W_r': 4.732,
     'L0_ffn_mu_r': 8.0,
     'L1_ffn_Wp': 8.0,
     'L1_ffn_sim': 8.0,
     'L1_ffn_Wd0': 8.0,
     'L1_ffn_Wu0': 8.0,
     'L1_ffn_Wd1': 8.0,
     'L1_ffn_Wu1': 8.0,
     'L1_ffn_Wd2': 8.0,
     'L1_ffn_Wu2': 8.0,
     'L1_ffn_Wd3': 8.0,
     'L1_ffn_Wu3': 8.0}
    for name, (base, spread) in spreads.items():
        noise = np.random.default_rng([zlib.crc32(name.encode()), seed]).standard_normal(out[name].shape)
        drawn = base * np.exp(spread * noise) if base else spread * noise
        out[name] = jnp.asarray(drawn.astype(out[name].dtype))
    for name, factor in factors.items():
        out[name] = (out[name] * factor).astype(out[name].dtype)
    return out
```

```python
import math
from contextlib import ExitStack

import numpy as np

import concourse.bass as bass
from concourse import mybir

F32 = mybir.dt.float32
F32R = mybir.dt.float32r
BF16 = mybir.dt.bfloat16
ALU = mybir.AluOpType
ACT = mybir.ActivationFunctionType
AX = mybir.AxisListType.X

P = 128
B, T, D = 8, 1024, 256
NB = B
H, DK = 16, 16
NT = T // P
KT = D // P
NP2 = NT // 2
CH = 512
NC = T // CH
G = 4
NG = H // G
HP = 32
PROJ = 64
RANKS = (1, 2, 4, 8)
NR = sum(RANKS)
NE = len(RANKS)
RW = PROJ + NR + NE
RS = 96
EPS = 1e-5
MASKED = -1e30
PAD = 8
TERMS = 4
MROW = TERMS * DK


def rope_table():
    inv = (1.0 / np.float32(10000.0) ** (np.arange(0, DK, 2, dtype=np.float32) / np.float32(DK))).astype(np.float32)
    freqs = np.outer(np.arange(T, dtype=np.float32), inv).astype(np.float32)
    emb = np.concatenate([freqs, freqs], -1)
    cos, sin = np.cos(emb), np.sin(emb)
    return np.stack([cos[:, 0::2].T, cos[:, 1::2].T, -sin[:, 0::2].T, sin[:, 1::2].T], axis=1).astype(np.float32)


def macaron(nc, a, out):
    ctx = ExitStack()
    with ctx:
        def sb(name, shape, dt=F32):
            return ctx.enter_context(nc.sbuf_tensor(name, shape, dt))

        def sem(name):
            return ctx.enter_context(nc.semaphore(name))

        wr0, wk0, wv0, wq1, wk1, wv1, wf1 = (
            sb(n, [P, KT, D]) for n in ("wr0", "wk0", "wv0", "wq1", "wk1", "wv1", "wf1"))
        wqkv = sb("wqkv", [P, KT, 3 * D])
        wo0 = sb("wo0", [P, NG, D])
        wo1 = sb("wo1", [P, NG, D])
        wroute = sb("wroute", [P, KT, RW])
        wup = sb("wup", [P, D])
        mu = sb("mu", [P, 2, 2, KT])
        bpb = sb("bpb", [P, PROJ])
        bsb = sb("bsb", [P, NE])
        first = sb("first", [P, NE])
        ident = sb("ident", [P, P])
        identb = sb("identb", [P, P], BF16)
        maskneg = sb("maskneg", [P, P], BF16)
        mask01 = sb("mask01", [P, P])
        hmask = sb("hmask", [P, H // KT])
        smask = sb("smask", [P, H // KT, HP])
        x = sb("x", [P, NT, D])
        xnT = sb("xnT", [P, KT, PAD + T])
        vpad = sb("vpad", [P, NT, H, HP])
        stq = [sb(f"stq{i}", [P, G, T], F32R) for i in range(2)]
        stk = [sb(f"stk{i}", [P, G, T], F32R) for i in range(2)]
        stats = sb("stats", [P, NT, 6])
        mv = sb("mv", [P, NT, 2])
        rstd = sb("rstd", [P, NT])
        small = sb("small", [P, 16, NT * NE])
        mhalf = sb("mhalf", [P, 2 * H])
        mxa = sb("mxa", [P, 2, G * NT])
        mxb = sb("mxb", [P, 2, G * NT // 2])
        mhi = sb("mhi", [G * NT, 2, P], F32R)
        mlo = sb("mlo", [G * NT, 2, P], F32R)

        KB = 256
        arena = sb("arena", [P, 74 * KB])

        def ar(at, *shape):
            n = math.prod(shape)
            v = arena[:, at * KB:at * KB + n]
            names = "abcd"[:len(shape)]
            return v.rearrange(f"p ({' '.join(names)}) -> p {' '.join(names)}", **dict(zip(names[1:], shape[1:]))) if len(shape) > 1 else v

        xm = [ar(0, KT, T), ar(8, KT, T)]
        kact = ar(16, KT, T)
        th = ar(24, NT, D)
        prod = ar(32, 2, 2, D)
        xns = [ar(0, NT, D)] * 4 + [ar(64, NT, D), ar(0, NT, D)]
        qT = ar(0, KT, T)
        khT = ar(8, KT, T)
        kh = ar(16, NT, D)
        qbd = ar(24, 2, H, P)
        scm = ar(40, G, CH)
        ksq = ar(48, 2, 2, D)
        ssb = ar(52, 2, NG, P)
        yT = ar(56, NG, T)
        kvar = ar(72, 2, 2, H)
        ropet = ar(0, 4, T)
        pexp = ar(0, 4, 2, CH)
        hl = [[ar(16 + 16 * q + 8 * i, 2, T) for i in range(2)] for q in range(2)]
        ra = ar(48, 2, 2, CH)
        rb = ar(64, 2, 2, CH)
        yrec = ar(52, CH)
        yshf = ar(54, CH)
        projb = ar(0, NT, PROJ)
        psq = ar(2, NT, PROJ)
        dg = ar(4, NT, HP)
        dgT = ar(5, NT, P)
        raw = ar(0, 7, KT, D)
        rawo = ar(14, KT, NG, G, HP)
        rawp = ar(18, D)
        rawd = ar(19, D)
        rawu = ar(20, KT, 4, HP)
        rsim = ar(22, 16, NE)
        rbp = ar(23, P)
        kmean = ar(24, KT, H)
        ones = ar(25, P)

        bank = [ctx.enter_context(nc.psum_tensor(f"bank{i}", [P, 2 * CH], F32)) for i in range(4)]

        def ps(i, n=1):
            return bank[i // 2][:, (i % 2) * CH:(i % 2) * CH + n * CH]

        mm = nc.tensor.matmul

        w_in, w_mem, w_pool, w_norm = sem("w_in"), sem("w_mem"), sem("w_pool"), sem("w_norm")
        w_tr, w_cp, w_dve, w_act, w_ps2 = sem("w_tr"), sem("w_cp"), sem("w_dve"), sem("w_act"), sem("w_ps2")
        rope_d = nc.inline_tensor(rope_table(), name="rope_table").ap()
        zero_d = nc.inline_tensor(np.zeros((2, G * T), np.float32), name="zero_rows").ap()

        NLOAD = 5 + 2 + 1 + G * (1 + KT) + 1 + NE * 5 + 2 + 1 + 3

        with nc.allow_non_contiguous_dma(reason="small weights, once"), nc.Block() as block:
            @block.sync
            def _(sp):
                n = 0

                def load(dst, src):
                    nonlocal n
                    sp.dma_start(dst, src).then_inc(w_in, 16)
                    n += 1

                sp.wait_ge(w_mem, 4)
                for i, w in enumerate((a["L0_ffn_W_r"], a["L0_ffn_W_k"], a["L0_ffn_W_v"], None, None, a["L1_attn_Wv"], a["L1_ffn_W"])):
                    if w is not None:
                        load(raw[:, i], w.rearrange("(k p) c -> p k c", p=P))
                for i, w in ((3, a["L1_attn_Wq"]), (4, a["L1_attn_Wk"])):
                    load(raw[:, i], w.rearrange("(m two) c -> m two c", two=2))
                load(wqkv[:], a["L0_attn_W_qkv"].rearrange("(k p) c -> p k c", p=P))
                for j in range(G):
                    load(wo0[HP * j:HP * j + DK], a["L0_attn_W_o"].rearrange("(g j d) o -> j d g o", g=NG, j=G)[j])
                    for k in range(KT):
                        load(rawo[:, k, :, j, 0:DK],
                             a["L1_attn_Wo"].rearrange("(k p) (g j d) -> k j p g d", k=KT, g=NG, j=G)[k, j])
                load(rawp[0:PROJ], a["L1_ffn_Wp"])
                r0 = 0
                for e, r in enumerate(RANKS):
                    load(rawd[r0:r0 + r], a[f"L1_ffn_Wd{e}"])
                    for j in range(4):
                        load(rawu[:, :, j, r0:r0 + r], a[f"L1_ffn_Wu{e}"].rearrange("(k p) r -> p k r", p=P))
                    r0 += r
                for m, w in enumerate((a["L0_ffn_mu_k"], a["L0_ffn_mu_r"])):
                    load(mu[:, m, 0, :], w.rearrange("(k p) -> p k", p=P))
                load(bpb[:], a["L1_ffn_bp"].partition_broadcast(P))
                load(rsim[0:PROJ, 0], a["L1_ffn_sim"])
                load(rsim[0:PROJ, 1, 0:1], a["L1_ffn_temp"].partition_broadcast(PROJ))
                load(rsim[0:PROJ, 2, 0:1], a["L1_ffn_bp"].rearrange("(p o) -> p o", o=1))
                assert n == NLOAD, n

            @block.gpsimd
            def _(pool):
                nc.gpsimd.memset(wo0[:], 0.0).then_inc(w_mem, 1)
                nc.gpsimd.memset(rawo[:], 0.0).then_inc(w_mem, 1)
                nc.gpsimd.memset(rawu[:], 0.0).then_inc(w_mem, 1)
                nc.gpsimd.memset(rawd[:], 0.0).then_inc(w_mem, 1)
                for t, v in ((ident, 0.0), (identb, 0.0), (maskneg, 0.0), (mask01, 1.0), (hmask, 1.0), (smask, 0.0),
                             (ones, 1.0)):
                    nc.gpsimd.memset(t[:], v).then_inc(w_pool, 1)
                nc.gpsimd.memset(xnT[:, :, 0:PAD], 0.0)
                nc.gpsimd.memset(vpad[:], 1.0)
                nc.gpsimd.memset(mhalf[:], -0.5)
                for e in range(NE):
                    nc.gpsimd.memset(first[:, e:e + 1], float(NE - e))
                pool.wait_ge(w_pool, 7)
                nc.gpsimd.memset(smask[:, :, 0:DK], 1.0).then_inc(w_pool, 1)

                def select(t, op, fill, base, pattern, cm):
                    return nc.gpsimd.affine_select(out=t, in_=t, compare_op=op, fill=fill, base=base,
                                                   pattern=pattern, channel_multiplier=cm)

                select(ident[:], ALU.not_equal, 1.0, 0, [[-1, P]], 1).then_inc(w_pool, 1)
                select(identb[:], ALU.not_equal, 1.0, 0, [[-1, P]], 1).then_inc(w_pool, 1)
                select(maskneg[:], ALU.is_ge, MASKED, 0, [[-1, P]], 1).then_inc(w_pool, 1)
                select(mask01[:], ALU.is_ge, 0.0, 0, [[1, P]], -1).then_inc(w_pool, 1)
                pool.wait_ge(w_pool, 8)
                for t, pat in ((hmask[:], [[-DK, H // KT]]), (smask[:], [[-DK, H // KT], [0, HP]])):
                    neg = [[-s, c] for s, c in pat]
                    select(t, ALU.is_ge, 0.0, 0, pat, 1).then_inc(w_pool, 1)
                    pool.wait_ge(w_pool, 13 if t is not None and len(pat) == 1 else 15)
                    select(t, ALU.is_ge, 0.0, DK - 1, neg, -1).then_inc(w_pool, 1)
                pool.wait_ge(w_dve, 4)
                nc.gpsimd.tensor_scalar(rsim[0:PROJ, 5], rsim[0:PROJ, 5], 1e-24, None, ALU.max).then_inc(w_norm, 1)
                pool.wait_ge(w_norm, 1)
                nc.gpsimd.tensor_tensor(rsim[0:PROJ, 5], rsim[0:PROJ, 5], mhalf[0:PROJ, 0:NE], ALU.pow).then_inc(w_norm, 1)

            @block.tensor
            def _(pe):
                pe.wait_ge(w_in, 16 * NLOAD)
                pe.wait_ge(w_pool, 9)
                for m in range(7):
                    for k in range(KT):
                        for o in range(KT):
                            src = raw[:, m, o, k * P:(k + 1) * P]
                            last = nc.tensor.transpose(ps(m)[:, k * D + o * P:k * D + (o + 1) * P], src, ident[:])
                    last.then_inc(w_tr, 1)
                for k in range(KT):
                    nc.tensor.transpose(ps(7)[:, k * PROJ:(k + 1) * PROJ], rawp[0:PROJ, k * P:(k + 1) * P],
                                        ident[0:PROJ, 0:PROJ])
                    nc.tensor.transpose(ps(7)[:, 128 + 16 * k:144 + 16 * k], rawd[0:16, k * P:(k + 1) * P],
                                        ident[0:16, 0:16])
                    last = nc.tensor.transpose(ps(7)[:, 160 + k * P:160 + (k + 1) * P],
                                               rawu[:, k].rearrange("p j r -> p (j r)"), ident[:])
                last.then_inc(w_tr, 1)
                pe.wait_ge(w_cp, 2)
                for g in range(NG):
                    for k in range(KT):
                        last = nc.tensor.transpose(ps(0, 2)[:, g * D + k * P:g * D + (k + 1) * P],
                                                   rawo[:, k, g].rearrange("p j r -> p (j r)"), ident[:])
                last.then_inc(w_tr, 1)
                pe.wait_ge(w_dve, 3)
                pe.wait_ge(w_cp, 5)
                mm(ps(2)[0:PROJ, 0:NE], ones[0:PROJ, 0:PROJ], rsim[0:PROJ, 3], start=True, stop=True).then_inc(w_ps2, 1)
                pe.wait_ge(w_dve, 7)
                for k in range(KT):
                    mm(ps(3)[:, 8 * k:8 * k + NE], rawp[0:PROJ, k * P:(k + 1) * P], rsim[0:PROJ, 6], start=True, stop=True)
                mm(ps(4)[:, 0:NE], rbp[0:PROJ, :], rsim[0:PROJ, 6], start=True, stop=True).then_inc(w_ps2, 1)

            @block.scalar
            def _(act):
                act.wait_ge(w_dve, 2)
                nc.scalar.activation(rsim[0:PROJ, 4, 0:1], rsim[0:PROJ, 4, 1:2], ACT.Exp).then_inc(w_act, 1)

            @block.vector
            def _(dve):
                dve.wait_ge(w_in, 16 * NLOAD)
                nc.vector.tensor_scalar(mu[:, :, 1, :], mu[:, :, 0, :], -1.0, 1.0, ALU.mult, ALU.add).then_inc(w_dve, 1)
                nc.vector.tensor_scalar(rsim[0:PROJ, 4, 1:2], rsim[0:PROJ, 1, 0:1], math.log(1.0 / 0.01), None,
                                        ALU.min).then_inc(w_dve, 1)
                nc.vector.tensor_tensor(rsim[0:PROJ, 3], rsim[0:PROJ, 0], rsim[0:PROJ, 0], ALU.mult).then_inc(w_dve, 1)
                for m, w in enumerate((wr0, wk0, wv0, wq1, wk1, wv1, wf1)):
                    dve.wait_ge(w_tr, m + 1)
                    nc.vector.tensor_copy(w[:].rearrange("p k c -> p (k c)"), ps(m)).then_inc(w_cp, 1)
                dve.wait_ge(w_tr, 8)
                nc.vector.tensor_copy(wroute[:, :, 0:PROJ], ps(7)[:, 0:128].rearrange("p (k c) -> p k c", k=KT))
                nc.vector.tensor_copy(wroute[:, :, PROJ:PROJ + NR], ps(7)[:, 128:160].rearrange("p (k c) -> p k c", k=KT)[:, :, 0:NR])
                nc.vector.tensor_copy(wup[:], ps(7)[:, 160:160 + D])
                dve.wait_ge(w_tr, 9)
                nc.vector.tensor_copy(wo1[:].rearrange("p g c -> p (g c)"), ps(0, 2))
                dve.wait_ge(w_ps2, 1)
                nc.vector.tensor_copy(rsim[0:PROJ, 5], ps(2)[0:PROJ, 0:NE]).then_inc(w_dve, 1)
                dve.wait_ge(w_act, 1)
                dve.wait_ge(w_norm, 2)
                nc.vector.scalar_tensor_tensor(out=rsim[0:PROJ, 7], in0=rsim[0:PROJ, 0], scalar=rsim[0:PROJ, 4, 0:1],
                                               in1=rsim[0:PROJ, 5], op0=ALU.mult, op1=ALU.mult).then_inc(w_dve, 1)
                dve.wait_ge(w_dve, 5)
                nc.vector.tensor_copy(rsim[0:PROJ, 6], rsim[0:PROJ, 7]).then_inc(w_dve, 1)
                dve.wait_ge(w_pool, 7)
                nc.vector.tensor_scalar(rbp[0:PROJ, :], ones[0:PROJ, :], rsim[0:PROJ, 2, 0:1], None, ALU.mult).then_inc(w_dve, 1)
                dve.wait_ge(w_ps2, 2)
                nc.vector.tensor_copy(wroute[:, :, PROJ + NR:RW], ps(3)[:, 0:16].rearrange("p (k c) -> p k c", k=KT)[:, :, 0:NE])
                nc.vector.tensor_copy(bsb[:], ps(4)[:, 0:NE])
                wk = wqkv[:, :, D:2 * D].rearrange("p k (h d) -> p k h d", h=H)
                for k in range(KT):
                    nc.vector.reduce_sum(kmean[:, k], wk[:, k], AX).then_inc(w_dve, 1)
                dve.wait_ge(w_dve, 9)
                for k in range(KT):
                    nc.vector.scalar_tensor_tensor(out=wk[:, k], in0=kmean[:, k].unsqueeze(2).broadcast_to([P, H, DK]),
                                                   scalar=-1.0 / DK, in1=wk[:, k], op0=ALU.mult, op1=ALU.add)
                for s in (*stq, *stk):
                    nc.vector.memset(s[MROW:P].bitcast(F32), 0.0).then_inc(w_dve, 1)
                dve.wait_ge(w_dve, 13)
                for s in stk:
                    nc.vector.memset(s[MROW:MROW + 2].bitcast(F32), 1.0)

        names = ("x_in x_out ln_stats ln_aggr ln_vareps ln_rstd xn_done xT_ps xT mix_t mix kT_ps relu_done kact_done r_ps th_done o_ps "
                 "prod_done x_upd q_ps qT_done qbd_done kv_ps ksq_done v_done kvar_done kvar_eps krs_done kh_done khT_ps khT_done "
                 "sc_ps sc_masked y_ps yT_done st_ps state_done oproj_ps rt_ps rt_floor rt_norm rt_step rt_act dgT_ps dgT_done base_ps "
                 "rope_in qk_ps rope_ab rope_r rope_hi rope_lo stack0 stack1 v1_ps v1_done s_ps smax_done mx_comb mT_ps "
                 "m_hl mrow0 mrow1 t_ps exp_done causal_done pv_done y_rec y_shf y_norm").split()
        s = {n: sem(n) for n in names}
        stack_in = [s["stack0"], s["stack1"]]
        max_in = [s["mrow0"], s["mrow1"]]

        with nc.Fori(0, NB) as it:
            with nc.Block() as block:
                def ln_dve(n):
                    for c in range(NC):
                        if n:
                            nc.vector.wait_ge(s["x_upd"], NP2 * (n - 1) + 2 * c + 2)
                        else:
                            nc.vector.wait_ge(s["x_in"], 16)
                        for t in range(4 * c, 4 * c + 4):
                            nc.vector.bn_stats(stats[:, t], x[:, t]).then_inc(s["ln_stats"], 1)
                        nc.vector.wait_ge(s["ln_stats"], NT * n + 4 * c + 4)
                        for t in range(4 * c, 4 * c + 4):
                            nc.vector.bn_aggr(mv[:, t], stats[:, t]).then_inc(s["ln_aggr"], 1)

                def ln_pool(n):
                    for t in range(NT):
                        if t % 4 == 0:
                            nc.gpsimd.wait_ge(s["ln_aggr"], NT * n + t + 4)
                            nc.gpsimd.tensor_scalar(rstd[:, t:t + 4], mv[:, t:t + 4, 1], EPS, None, ALU.add).then_inc(s["ln_vareps"], 1)
                            nc.gpsimd.wait_ge(s["ln_vareps"], NC * n + t // 4 + 1)
                            nc.gpsimd.tensor_tensor(rstd[:, t:t + 4], rstd[:, t:t + 4], mhalf[:, 0:4], ALU.pow).then_inc(s["ln_rstd"], 1)
                            nc.gpsimd.wait_ge(s["ln_rstd"], NC * n + t // 4 + 1)
                        nc.gpsimd.tensor_scalar(xns[n][:, t], x[:, t], mv[:, t, 0:1], rstd[:, t:t + 1], ALU.subtract,
                                                ALU.mult).then_inc(s["xn_done"], 1)

                def ln_pe(n):
                    for t in range(NT):
                        c = t // 4
                        nc.tensor.wait_ge(s["xn_done"], NT * n + t + 1)
                        for k in range(KT):
                            last = nc.tensor.transpose(ps(2 * c + k)[:, (t % 4) * P:(t % 4 + 1) * P],
                                                       xns[n][:, t, k * P:(k + 1) * P], ident[:])
                            if t % 4 == 3:
                                last.then_inc(s["xT_ps"], 1)

                def ln_act(n):
                    for c in range(NC):
                        for k in range(KT):
                            nc.scalar.wait_ge(s["xT_ps"], 4 * n + 2 * c + k + 1)
                            nc.scalar.copy(xnT[:, k, PAD + CH * c:PAD + CH * (c + 1)], ps(2 * c + k)).then_inc(s["xT"], 1)

                def xT_ready(eng, n, c=NC - 1):
                    eng.wait_ge(s["xT"], 4 * n + 2 * c + 2)

                def tok(t):
                    return slice(PAD + t * P, PAD + (t + 1) * P)

                def ffn_pool(f, n):
                    xT_ready(nc.gpsimd, n)
                    for m in range(2):
                        for k in range(KT):
                            nc.gpsimd.tensor_scalar(xm[m][:, k], xnT[:, k, PAD - 1:PAD - 1 + T], mu[:, m, 1, k:k + 1], None,
                                                    ALU.mult).then_inc(s["mix_t"], 1)
                    for c in range(NC):
                        nc.gpsimd.wait_ge(s["relu_done"], 4 * f + 2 * c + 2)
                        v = kact[:, :, c * CH:(c + 1) * CH]
                        nc.gpsimd.tensor_tensor(v, v, v, ALU.mult).then_inc(s["kact_done"], 1)

                def ffn_dve(f, n, src_dst_stage):
                    for m in range(2):
                        for k in range(KT):
                            nc.vector.wait_ge(s["mix_t"], 4 * f + 2 * m + k + 1)
                            nc.vector.scalar_tensor_tensor(out=xm[m][:, k], in0=xnT[:, k, PAD:PAD + T], scalar=mu[:, m, 0, k:k + 1],
                                                           in1=xm[m][:, k], op0=ALU.mult, op1=ALU.add).then_inc(s["mix"], 1)
                    for p in range(NP2):
                        nc.vector.wait_ge(s["th_done"], NP2 * f + p + 1)
                        nc.vector.wait_ge(s["o_ps"], NP2 * f + p + 1)
                        nc.vector.scalar_tensor_tensor(out=prod[:, p % 2].rearrange("p t c -> p (t c)"),
                                                       in0=th[:, 2 * p:2 * p + 2].rearrange("p t c -> p (t c)"), scalar=1.0, in1=ps(4 + p),
                                                       op0=ALU.add, op1=ALU.mult).then_inc(s["prod_done"], 1)
                        nc.vector.wait_ge(s["prod_done"], NP2 * f + p + 1)
                        xv = x[:, 2 * p:2 * p + 2]
                        nc.vector.scalar_tensor_tensor(out=xv, in0=prod[:, p % 2], scalar=0.25, in1=xv, op0=ALU.mult,
                                                       op1=ALU.add).then_inc(s["x_upd"], 1)

                def ffn_pe(f, n):
                    nc.tensor.wait_ge(s["mix"], 4 * f + 2)
                    for c in range(NC):
                        for m in range(KT):
                            for k in range(KT):
                                last = mm(ps(4 + 2 * c + m), wk0[:, k, m * P:(m + 1) * P], xm[0][:, k, c * CH:(c + 1) * CH],
                                          start=k == 0, stop=k == KT - 1)
                            last.then_inc(s["kT_ps"], 1)
                    nc.tensor.wait_ge(s["mix"], 4 * f + 4)
                    for p in range(NP2):
                        for i in range(2):
                            for k in range(KT):
                                last = mm(ps(p)[:, i * D:(i + 1) * D], xm[1][:, k, (2 * p + i) * P:(2 * p + i + 1) * P], wr0[:, k],
                                          start=k == 0, stop=k == KT - 1)
                        last.then_inc(s["r_ps"], 1)
                    for p in range(NP2):
                        nc.tensor.wait_ge(s["kact_done"], NC * f + p // 2 + 1)
                        for i in range(2):
                            for k in range(KT):
                                last = mm(ps(4 + p)[:, i * D:(i + 1) * D], kact[:, k, (2 * p + i) * P:(2 * p + i + 1) * P], wv0[:, k],
                                          start=k == 0, stop=k == KT - 1)
                        last.then_inc(s["o_ps"], 1)

                def ffn_act(f, n):
                    for c in range(NC):
                        for m in range(KT):
                            nc.scalar.wait_ge(s["kT_ps"], 4 * f + 2 * c + m + 1)
                            nc.scalar.activation(kact[:, m, c * CH:(c + 1) * CH], ps(4 + 2 * c + m), ACT.Relu).then_inc(s["relu_done"], 1)
                    for p in range(NP2):
                        nc.scalar.wait_ge(s["r_ps"], NP2 * f + p + 1)
                        nc.scalar.activation(th[:, 2 * p:2 * p + 2].rearrange("p t c -> p (t c)"), ps(p), ACT.Tanh,
                                             scale=0.5).then_inc(s["th_done"], 1)

                def lin_pe():
                    for c in range(NC):
                        xT_ready(nc.tensor, 1, c)
                        for m in range(KT):
                            for k in range(KT):
                                last = mm(ps(4 + 2 * c + m), wqkv[:, k, m * P:(m + 1) * P],
                                          xnT[:, k, PAD + c * CH:PAD + (c + 1) * CH], start=k == 0, stop=k == KT - 1)
                            last.then_inc(s["q_ps"], 1)
                    for p in range(NP2):
                        if p >= 2:
                            nc.tensor.wait_ge(s["kh_done"], p - 1)
                            nc.tensor.wait_ge(s["v_done"], p - 1)
                        for i in range(2):
                            for k in range(KT):
                                last = mm(ps(2 * (p % 2) + i), xnT[:, k, tok(2 * p + i)], wqkv[:, k, D:3 * D], start=k == 0,
                                          stop=k == KT - 1)
                        last.then_inc(s["kv_ps"], 1)
                    for t in range(NT):
                        nc.tensor.wait_ge(s["kh_done"], t // 2 + 1)
                        nc.tensor.wait_ge(s["qT_done"], 2 * (t // 4) + 2)
                        for k in range(KT):
                            last = nc.tensor.transpose(ps(4 + 2 * (t // 4) + k)[:, (t % 4) * P:(t % 4 + 1) * P],
                                                       kh[:, t, k * P:(k + 1) * P], ident[:])
                            if t % 4 == 3:
                                last.then_inc(s["khT_ps"], 1)
                    nc.tensor.wait_ge(s["v_done"], NP2)

                    def scores(t):
                        nc.tensor.wait_ge(s["khT_done"], 2 * (t // 4) + 2)
                        for g in range(NG):
                            u = NG * t + g
                            nc.tensor.wait_ge(s["qbd_done"], H * t + G * g + G)
                            if u >= 2:
                                nc.tensor.wait_ge(s["sc_masked"], u - 1)
                            mm(ps(u % 2), khT[:, g // 2, t * P:(t + 1) * P],
                               qbd[:, t % 2, G * g:G * g + G], start=True, stop=True).then_inc(s["sc_ps"], 1)

                    scores(0)
                    for t in range(NT):
                        if t < NT - 1:
                            if t:
                                nc.tensor.wait_ge(s["state_done"], t)
                            for g in range(NG):
                                last = mm(ps(4)[:, g * P:(g + 1) * P], kh[:, t, (g // 2) * P:(g // 2 + 1) * P],
                                          vpad[:, t, G * g:G * g + G], start=t == 0 and g == 0, stop=t == NT - 2,
                                          skip_group_check=True)
                            last.then_inc(s["st_ps"], 1)
                        y = ps(2 + t % 2)
                        if t >= 2:
                            nc.tensor.wait_ge(s["yT_done"], t - 1)
                        for g in range(NG):
                            if t:
                                nc.tensor.wait_ge(s["state_done"], t)
                                mm(y[:, g * P:(g + 1) * P], ssb[:, (t - 1) % 2, g], qT[:, g // 2, t * P:(t + 1) * P], start=True,
                                   stop=False, skip_group_check=True)
                            nc.tensor.wait_ge(s["sc_masked"], NG * t + g + 1)
                            for j in range(G):
                                last = mm(y[HP * j:HP * (j + 1), g * P:(g + 1) * P], vpad[:, t, G * g + j],
                                          scm[:, g, j * P:(j + 1) * P], start=t == 0, stop=True, skip_group_check=True,
                                          tile_position=(0, HP * j))
                        last.then_inc(s["y_ps"], 1)
                        if t < NT - 1:
                            scores(t + 1)
                    attn_out_pe(0, wo0, 4, lambda t: nc.tensor.wait_ge(s["yT_done"], t + 1))

                def attn_out_pe(n, w, b0, ready):
                    for p in range(NP2):
                        for i in range(2):
                            ready(2 * p + i)
                            for g in range(NG):
                                last = mm(ps(b0 + p)[:, i * D:(i + 1) * D], yT[:, g, (2 * p + i) * P:(2 * p + i + 1) * P], w[:, g],
                                          start=g == 0, stop=g == NG - 1)
                        last.then_inc(s["oproj_ps"], 1)

                def attn_out_dve(n, stage, b0):
                    for p in range(NP2):
                        nc.vector.wait_ge(s["oproj_ps"], NP2 * n + p + 1)
                        xv = x[:, 2 * p:2 * p + 2]
                        nc.vector.tensor_tensor(xv, xv, ps(b0 + p).rearrange("p (t c) -> p t c", t=2), ALU.add).then_inc(s["x_upd"], 1)

                def lin_act():
                    for c in range(NC):
                        for m in range(KT):
                            nc.scalar.wait_ge(s["q_ps"], 2 * c + m + 1)
                            nc.scalar.copy(qT[:, m, c * CH:(c + 1) * CH], ps(4 + 2 * c + m)).then_inc(s["qT_done"], 1)
                    for p in range(NP2):
                        nc.scalar.wait_ge(s["kv_ps"], p + 1)
                        if p >= 2:
                            nc.scalar.wait_ge(s["kvar_done"], p - 1)
                        kv = ps(2 * (p % 2), 2).rearrange("p (t c) -> p t c", t=2)
                        nc.scalar.copy(vpad[:, 2 * p:2 * p + 2, :, 0:DK],
                                       kv[:, :, D:2 * D].rearrange("p t (h d) -> p t h d", h=H)).then_inc(s["v_done"], 1)
                        nc.scalar.activation(ksq[:, p % 2], kv[:, :, 0:D], ACT.Square).then_inc(s["ksq_done"], 1)
                    for c in range(NC):
                        for k in range(KT):
                            nc.scalar.wait_ge(s["khT_ps"], 2 * c + k + 1)
                            nc.scalar.copy(khT[:, k, c * CH:(c + 1) * CH], ps(4 + 2 * c + k)).then_inc(s["khT_done"], 1)
                    for t in range(NT):
                        nc.scalar.wait_ge(s["y_ps"], t + 1)
                        nc.scalar.copy(yT[:, :, t * P:(t + 1) * P], ps(2 + t % 2).rearrange("p (g c) -> p g c", g=NG)).then_inc(s["yT_done"], 1)

                def lin_pool():
                    for p in range(NP2):
                        nc.gpsimd.wait_ge(s["kvar_done"], p + 1)
                        v = kvar[:, p % 2].rearrange("p t h -> p (t h)")
                        nc.gpsimd.tensor_scalar(v, v, DK * EPS, None, ALU.add).then_inc(s["kvar_eps"], 1)
                        nc.gpsimd.wait_ge(s["kvar_eps"], p + 1)
                        nc.gpsimd.tensor_tensor(v, v, mhalf[:], ALU.pow).then_inc(s["krs_done"], 1)
                    for t in range(NT):
                        nc.gpsimd.wait_ge(s["qT_done"], 2 * (t // 4) + 2)
                        if t >= 2:
                            nc.gpsimd.wait_ge(s["sc_ps"], NG * (t - 1))
                        for h in range(H):
                            nc.gpsimd.tensor_scalar(qbd[:, t % 2, h], qT[:, h // 8, t * P:(t + 1) * P], hmask[:, h % 8:h % 8 + 1],
                                                    None, ALU.mult).then_inc(s["qbd_done"], 1)

                def lin_dve():
                    for p in range(NP2):
                        nc.vector.wait_ge(s["ksq_done"], p + 1)
                        nc.vector.reduce_sum(kvar[:, p % 2].rearrange("p t h -> p (t h)"),
                                             ksq[:, p % 2].rearrange("p t (h d) -> p (t h) d", h=H), AX).then_inc(s["kvar_done"], 1)
                        nc.vector.wait_ge(s["krs_done"], p + 1)
                        for i in range(2):
                            last = nc.vector.scalar_tensor_tensor(
                                out=kh[:, 2 * p + i].rearrange("p (h d) -> p h d", h=H),
                                in0=ps(2 * (p % 2) + i)[:, 0:D].rearrange("p (h d) -> p h d", h=H), scalar=math.sqrt(DK),
                                in1=kvar[:, p % 2, i].unsqueeze(2).broadcast_to([P, H, DK]), op0=ALU.mult, op1=ALU.mult)
                        last.then_inc(s["kh_done"], 1)
                    for t in range(NT):
                        for g in range(NG):
                            nc.vector.wait_ge(s["sc_ps"], NG * t + g + 1)
                            if t:
                                nc.vector.wait_ge(s["y_ps"], t)
                            nc.vector.tensor_tensor(scm[:, g].rearrange("p (j c) -> p j c", j=G),
                                                    ps((NG * t + g) % 2).rearrange("p (j c) -> p j c", j=G),
                                                    mask01[:].unsqueeze(1).broadcast_to([P, G, P]), ALU.mult).then_inc(s["sc_masked"], 1)
                        if t < NT - 1:
                            nc.vector.wait_ge(s["st_ps"], t + 1)
                            nc.vector.tensor_tensor(ssb[:, t % 2].rearrange("p (a b) c -> p a (b c)", a=2),
                                                    ps(4).rearrange("p (a c) -> p a c", a=2),
                                                    smask[:].rearrange("p h c -> p (h c)").unsqueeze(1).broadcast_to([P, 2, 2 * P]),
                                                    ALU.mult).then_inc(s["state_done"], 1)
                    attn_out_dve(0, 1, 4)

                def exp_pe(g, n):
                    for t in range(NT):
                        xT_ready(nc.tensor, n, t // 4)
                        for k in range(KT):
                            last = mm(ps(4 + t // 4)[:, (t % 4) * RS:(t % 4) * RS + RW], xnT[:, k, tok(t)], wroute[:, k],
                                      start=k == 0, stop=k == KT - 1)
                        if t % 4 == 3:
                            last.then_inc(s["rt_ps"], 1)
                    for t in range(NT):
                        for k in range(KT):
                            mm(ps(t // 2)[:, (t % 2) * D:(t % 2 + 1) * D], xnT[:, k, tok(t)], wf1[:, k], start=k == 0 and t % 2 == 0,
                               stop=False, skip_group_check=True)
                    nc.tensor.wait_ge(s["rt_step"], RSTEPS * (g + 1))
                    for t in range(NT):
                        last = nc.tensor.transpose(ps(6, 2)[0:NR, t * P:(t + 1) * P], dg[:, t, 0:NR], ident[:])
                    last.then_inc(s["dgT_ps"], 1)
                    nc.tensor.wait_ge(s["dgT_done"], g + 1)
                    for t in range(NT):
                        last = mm(ps(t // 2)[:, (t % 2) * D:(t % 2 + 1) * D], dgT[0:NR, t], wup[0:NR], start=False, stop=True,
                                  skip_group_check=True)
                        if t % 2:
                            last.then_inc(s["base_ps"], 1)

                def exp_pool(g):
                    nc.gpsimd.wait_ge(s["rt_step"], RSTEPS * g + 3)
                    nc.gpsimd.tensor_scalar(small[:, 1, 0:NT], small[:, 1, 0:NT], 1e-24, None, ALU.max).then_inc(s["rt_floor"], 1)
                    nc.gpsimd.wait_ge(s["rt_floor"], g + 1)
                    nc.gpsimd.tensor_tensor(small[:, 1, 0:NT], small[:, 1, 0:NT], mhalf[:, 0:NT], ALU.pow).then_inc(s["rt_norm"], 1)

                def exp_act(g, n):
                    nc.scalar.wait_ge(s["rt_step"], RSTEPS * g + 1)
                    nc.scalar.activation(psq[:], projb[:], ACT.Square).then_inc(s["rt_act"], 1)
                    nc.scalar.wait_ge(s["rt_step"], RSTEPS * g + 6)
                    nc.scalar.activation(small[:, 4], small[:, 3], ACT.Exp).then_inc(s["rt_act"], 1)
                    nc.scalar.wait_ge(s["dgT_ps"], g + 1)
                    nc.scalar.copy(dgT[0:NR].rearrange("p q c -> p (q c)"), ps(6, 2)[0:NR, :]).then_inc(s["dgT_done"], 1)

                RSTEPS = 17

                def exp_dve(g, n, stage):
                    step = [RSTEPS * g]

                    def then(ins, wait=True):
                        step[0] += 1
                        ins.then_inc(s["rt_step"], 1)
                        if wait:
                            nc.vector.wait_ge(s["rt_step"], step[0])

                    def row(i, shape=None):
                        return small[:, i].rearrange("p (t e) -> p t e", t=NT)

                    def one(i):
                        return small[:, i, 0:NT]

                    def over(v):
                        return v.unsqueeze(2).broadcast_to([P, NT, NE])

                    rt = ps(4, 2).rearrange("p (b c) -> p b c", b=2)[:, :, 0:4 * RS].rearrange("p b (t c) -> p b t c", t=4)
                    nc.vector.wait_ge(s["rt_ps"], 2 * g + 2)
                    for b in range(2):
                        last = nc.vector.tensor_tensor(projb[:, 4 * b:4 * b + 4], rt[:, b, :, 0:PROJ],
                                                       bpb[:].unsqueeze(1).broadcast_to([P, 4, PROJ]), ALU.add)
                    then(last, False)
                    for b in range(2):
                        last = nc.vector.tensor_tensor(row(0)[:, 4 * b:4 * b + 4], rt[:, b, :, PROJ + NR:RW],
                                                       bsb[:].unsqueeze(1).broadcast_to([P, 4, NE]), ALU.add)
                    then(last, False)
                    nc.vector.wait_ge(s["rt_act"], 2 * g + 1)
                    then(nc.vector.reduce_sum(one(1), psq[:], AX), False)
                    nc.vector.wait_ge(s["rt_norm"], g + 1)
                    then(nc.vector.tensor_tensor(row(0), row(0), over(one(1)), ALU.mult))
                    then(nc.vector.reduce_max(one(2), row(0), AX))
                    then(nc.vector.tensor_tensor(row(3), row(0), over(one(2)), ALU.subtract))
                    then(nc.vector.tensor_scalar(row(5), row(3), 0.0, None, ALU.is_equal))
                    then(nc.vector.tensor_tensor(row(5), row(5), first[:].unsqueeze(1).broadcast_to([P, NT, NE]), ALU.mult))
                    then(nc.vector.reduce_max(one(6), row(5), AX))
                    then(nc.vector.tensor_tensor(row(7), row(5), over(one(6)), ALU.is_equal))
                    nc.vector.wait_ge(s["rt_act"], 2 * g + 2)
                    then(nc.vector.reduce_sum(one(8), row(4), AX))
                    then(nc.vector.reciprocal(one(9), one(8)))
                    then(nc.vector.tensor_tensor(row(10), row(7), over(one(9)), ALU.mult))
                    r0 = 0
                    for e, r in enumerate(RANKS):
                        for b in range(2):
                            last = nc.vector.tensor_tensor(dg[:, 4 * b:4 * b + 4, r0:r0 + r], rt[:, b, :, PROJ + r0:PROJ + r0 + r],
                                                           row(10)[:, 4 * b:4 * b + 4, e:e + 1].broadcast_to([P, 4, r]), ALU.mult)
                        then(last, False)
                        r0 += r
                    assert step[0] == RSTEPS * (g + 1)
                    for p in range(NP2):
                        nc.vector.wait_ge(s["base_ps"], NP2 * g + p + 1)
                        xv = x[:, 2 * p:2 * p + 2]
                        nc.vector.scalar_tensor_tensor(out=xv, in0=ps(p).rearrange("p (t c) -> p t c", t=2), scalar=0.5, in1=xv,
                                                       op0=ALU.mult, op1=ALU.add).then_inc(s["x_upd"], 1)

                ND = 2 * TERMS * 2
                tunits = [(c, kb, hp) for c in range(NC) for kb in range(4 * (c + 1)) for hp in range(2)]
                NTU = len(tunits)
                sunits = [(h, qb, k0, min(P * (qb + 1), k0 + CH)) for h in range(G) for qb in range(NT)
                          for k0 in range(0, P * (qb + 1), CH)]
                NSU = len(sunits)
                PER = 3
                MT_AT = NSU // PER + 1
                DIAG = [u for u, (c, kb, hp) in enumerate(tunits) if kb >= 4 * c]

                def width(c, kb):
                    return CH - max(0, kb - 4 * c) * P

                def sm_sync():
                    sp = nc.sync
                    sp.wait_ge(s["x_upd"], 4 * NP2)
                    sp.dma_start(ropet[:].rearrange("p a t -> p (a t)"),
                                 rope_d.rearrange("i a t -> i (a t)").partition_broadcast(H)).then_inc(s["rope_in"], 16)
                    for g in range(NG):
                        b = g % 2
                        sp.wait_ge(s["rope_lo"], 2 * NC)
                        if g >= 2:
                            sp.wait_ge(s["t_ps"], NTU * (g - 1))
                        sp.dma_start(stq[b][MROW:MROW + 2].bitcast(F32).rearrange("p h t -> p (h t)"), zero_d).then_inc(stack_in[b], 16)
                        for qk, st, halves in ((0, stq[b], (0, 0, 1, 1)), (1, stk[b], (0, 1, 0, 1))):
                            for term, half in enumerate(halves):
                                for o in range(2):
                                    r = DK * term + 8 * o
                                    for j in range(G):
                                        h = G * g + j
                                        sp.dma_start(st[r:r + 8, j].bitcast(F32), hl[qk][half][8 * h:8 * h + 8, o]).then_inc(stack_in[b], 16)
                        if g >= 1:
                            max_rows(g - 1)
                    max_rows(NG - 1)

                def max_rows(g):
                    nc.sync.wait_ge(s["m_hl"], 2 * g + 2)
                    for i, m in enumerate((mhi, mlo)):
                        nc.sync.dma_start(stq[g % 2][MROW + i:MROW + i + 1].bitcast(F32).rearrange("o h t -> o (h t)"),
                                          m[:, g % 2].bitcast(F32)).then_inc(max_in[g % 2], 16)

                def sm_pe():
                    for c in range(NC):
                        xT_ready(nc.tensor, 4, c)
                        for qk, w in enumerate((wq1, wk1)):
                            u = 2 * c + qk
                            if u >= 2:
                                nc.tensor.wait_ge(s["rope_ab"], 3 * (u - 1))
                            for m in range(KT):
                                for k in range(KT):
                                    last = mm(ps(4 + 2 * (u % 2) + m), w[:, k, m * P:(m + 1) * P], xnT[:, k, PAD + c * CH:PAD + (c + 1) * CH],
                                              start=k == 0, stop=k == KT - 1)
                            last.then_inc(s["qk_ps"], 1)
                    for p in range(NP2):
                        for i in range(2):
                            for k in range(KT):
                                last = mm(ps(p)[:, i * D:(i + 1) * D], xnT[:, k, tok(2 * p + i)], wv1[:, k], start=k == 0, stop=k == KT - 1)
                        last.then_inc(s["v1_ps"], 1)

                    def score(g, i):
                        h, qb, k0, k1 = sunits[i]
                        u = NSU * g + i
                        if i == 0:
                            nc.tensor.wait_ge(stack_in[g % 2], 16 * (ND * G + 1) * (g // 2 + 1))
                        if u >= 2:
                            nc.tensor.wait_ge(s["smax_done"], u - 1)
                        diag = k1 == P * (qb + 1)
                        last = mm(ps(6 + u % 2)[:, 0:k1 - k0], stq[g % 2][:, h, qb * P:(qb + 1) * P], stk[g % 2][:, h, k0:k1],
                                  start=True, stop=not diag)
                        if diag:
                            last = mm(ps(6 + u % 2)[:, k1 - k0 - P:k1 - k0], identb[:], maskneg[:], start=False, stop=True)
                        last.then_inc(s["s_ps"], 1)

                    def max_transpose(g):
                        nc.tensor.wait_ge(s["mx_comb"], g + 1)
                        nc.tensor.transpose(ps(6)[0:G * NT, 0:P], mxa[:, g % 2], ident[:]).then_inc(s["mT_ps"], 1)

                    def tscore(g, i):
                        c, kb, hp = tunits[i]
                        u = NTU * g + i
                        if i == 0:
                            nc.tensor.wait_ge(max_in[g % 2], 32 * (g // 2 + 1))
                        if u >= 2:
                            nc.tensor.wait_ge(s["exp_done"], u - 1)
                        n = width(c, kb)
                        for j in range(2):
                            last = mm(ps(2 * (u % 2) + j)[:, 0:n], stk[g % 2][:, 2 * hp + j, kb * P:(kb + 1) * P],
                                      stq[g % 2][:, 2 * hp + j, (c + 1) * CH - n:(c + 1) * CH], start=True, stop=True)
                        last.then_inc(s["t_ps"], 1)

                    def values(g, i):
                        c, kb, hp = tunits[i]
                        u = NTU * g + i
                        yu = NC * g + c
                        n = width(c, kb)
                        nc.tensor.wait_ge(s["exp_done"], u + 1)
                        if i in DIAG:
                            nc.tensor.wait_ge(s["causal_done"], len(DIAG) * g + DIAG.index(i) + 1)
                        if kb == 0 and hp == 0 and yu >= 2:
                            nc.tensor.wait_ge(s["y_norm"], yu - 1)
                        for j in range(2):
                            q = HP * (2 * hp + j)
                            last = mm(ps(4 + yu % 2)[q:q + HP, CH - n:CH], vpad[:, kb, G * g + 2 * hp + j], pexp[:, u % 4, j, 0:n],
                                      start=kb == 0, stop=kb == 4 * c + 3, tile_position=(0, q))
                        last.then_inc(s["pv_done"], 1)

                    for i in range(NSU):
                        score(0, i)
                    max_transpose(0)
                    nc.tensor.wait_ge(s["v1_done"], NP2)
                    for g in range(NG):
                        tscore(g, 0)
                        for i in range(NTU):
                            if i + 1 < NTU:
                                tscore(g, i + 1)
                            if g + 1 < NG:
                                for k in range(PER * i, min(PER * (i + 1), NSU)):
                                    score(g + 1, k)
                                if i == MT_AT:
                                    max_transpose(g + 1)
                            values(g, i)
                    attn_out_pe(1, wo1, 0, lambda t: nc.tensor.wait_ge(s["y_norm"], NC * NG) if t == 0 else None)

                def sm_dve():
                    nc.vector.wait_ge(s["rope_in"], 16)
                    for u in range(2 * NC):
                        c = u // 2
                        cs = slice(c * CH, (c + 1) * CH)
                        nc.vector.wait_ge(s["qk_ps"], u + 1)
                        if u >= 2:
                            nc.vector.wait_ge(s["rope_lo"], u - 1)
                        src = ps(4 + 2 * (u % 2), 2).rearrange("p (o c) -> p o c", o=2)
                        nc.vector.tensor_tensor(ra[:, u % 2], src, ropet[:, 0:2, cs], ALU.mult).then_inc(s["rope_ab"], 1)
                        for o in range(2):
                            nc.vector.tensor_tensor(rb[:, u % 2, o], src[:, 1 - o], ropet[:, 2 + o, cs], ALU.mult).then_inc(s["rope_ab"], 1)

                    def maxima(g, i):
                        h, qb, k0, k1 = sunits[i]
                        u = NSU * g + i
                        dst = mxa[:, g % 2, NT * h + qb:NT * h + qb + 1] if k0 == 0 else mxb[:, g % 2, 4 * h + qb - 4:4 * h + qb - 3]
                        nc.vector.wait_ge(s["s_ps"], u + 1)
                        nc.vector.reduce_max(dst, ps(6 + u % 2)[:, 0:k1 - k0], AX).then_inc(s["smax_done"], 1)

                    def negate(g):
                        nc.vector.wait_ge(s["smax_done"], NSU * (g + 1))
                        late = mxa[:, g % 2].rearrange("p (h q) -> p h q", h=G)[:, :, NT // 2:NT]
                        nc.vector.tensor_tensor(late, late, mxb[:, g % 2].rearrange("p (h q) -> p h q", h=G), ALU.max).then_inc(s["mx_comb"], 1)
                        nc.vector.wait_ge(s["mT_ps"], g + 1)
                        if g >= 2:
                            nc.vector.wait_ge(max_in[g % 2], 32 * (g // 2))
                        nc.vector.tensor_scalar(mhi[:, g % 2], ps(6)[0:G * NT, 0:P], -1.0, None, ALU.mult).then_inc(s["m_hl"], 1)
                        nc.vector.wait_ge(s["m_hl"], 2 * g + 1)
                        nc.vector.scalar_tensor_tensor(out=mlo[:, g % 2], in0=ps(6)[0:G * NT, 0:P], scalar=-1.0,
                                                       in1=mhi[:, g % 2].bitcast(F32), op0=ALU.mult, op1=ALU.subtract).then_inc(s["m_hl"], 1)

                    def finish(g, c):
                        yu = NC * g + c
                        nc.vector.wait_ge(s["pv_done"], NTU * g + (8 if c == 0 else NTU))
                        nc.vector.reciprocal(yrec[:], ps(4 + yu % 2)).then_inc(s["y_rec"], 1)
                        nc.vector.wait_ge(s["y_rec"], yu + 1)
                        nc.vector.stream_shuffle(yshf[:], yrec[:], [DK + i % DK for i in range(HP)]).then_inc(s["y_shf"], 1)
                        nc.vector.wait_ge(s["y_shf"], yu + 1)
                        nc.vector.tensor_tensor(yT[:, g, c * CH:(c + 1) * CH], ps(4 + yu % 2), yshf[:], ALU.mult).then_inc(s["y_norm"], 1)

                    for i in range(NSU):
                        maxima(0, i)
                    negate(0)
                    for g in range(NG):
                        for i in range(NTU):
                            if g + 1 < NG:
                                for k in range(PER * i, min(PER * (i + 1), NSU)):
                                    maxima(g + 1, k)
                                if i == MT_AT:
                                    negate(g + 1)
                            if i == 8:
                                finish(g, 0)
                        finish(g, 1)
                    attn_out_dve(1, 4, 0)

                def sm_act():
                    for u in range(2 * NC):
                        c, qk = u // 2, u % 2
                        nc.scalar.wait_ge(s["rope_r"], u + 1)
                        nc.scalar.copy(hl[qk][0][:, :, c * CH:(c + 1) * CH].bitcast(F32R), ra[:, u % 2]).then_inc(s["rope_hi"], 1)
                    for p in range(NP2):
                        nc.scalar.wait_ge(s["v1_ps"], p + 1)
                        nc.scalar.copy(vpad[:, 2 * p:2 * p + 2, :, 0:DK],
                                       ps(p).rearrange("p (t h d) -> p t h d", t=2, h=H)).then_inc(s["v1_done"], 1)
                    for g in range(NG):
                        for i, (c, kb, hp) in enumerate(tunits):
                            u = NTU * g + i
                            n = width(c, kb)
                            nc.scalar.wait_ge(s["t_ps"], u + 1)
                            if u >= 4:
                                nc.scalar.wait_ge(s["pv_done"], u - 3)
                            nc.scalar.activation(pexp[:, u % 4, :, 0:n], ps(2 * (u % 2), 2).rearrange("p (j c) -> p j c", j=2)[:, :, 0:n],
                                                 ACT.Exp, scale=DK ** -0.5).then_inc(s["exp_done"], 1)

                def sm_pool():
                    for u in range(2 * NC):
                        c, qk = u // 2, u % 2
                        nc.gpsimd.wait_ge(s["rope_ab"], 3 * (u + 1))
                        nc.gpsimd.tensor_tensor(ra[:, u % 2], ra[:, u % 2], rb[:, u % 2], ALU.add).then_inc(s["rope_r"], 1)
                        nc.gpsimd.wait_ge(s["rope_hi"], u + 1)
                        cs = slice(c * CH, (c + 1) * CH)
                        nc.gpsimd.tensor_tensor(hl[qk][1][:, :, cs].bitcast(F32R), ra[:, u % 2], hl[qk][0][:, :, cs], ALU.subtract).then_inc(s["rope_lo"], 1)
                    for g in range(NG):
                        for i in DIAG:
                            u = NTU * g + i
                            nc.gpsimd.wait_ge(s["exp_done"], u + 1)
                            v = pexp[:, u % 4, :, 0:P]
                            nc.gpsimd.affine_select(out=v, in_=v, compare_op=ALU.is_ge, fill=0.0, base=0, pattern=[[0, 2], [1, P]],
                                                    channel_multiplier=-1).then_inc(s["causal_done"], 1)

                def batch(dram):
                    return dram.rearrange("b t c -> (b t) c")[bass.ds(it * T, T)].rearrange("(t p) c -> p t c", p=P)

                @block.sync
                def _(sp):
                    sp.dma_start(x[:], batch(a["L0_attn_x"])).then_inc(s["x_in"], 16)
                    sm_sync()
                    sp.wait_ge(s["x_upd"], 6 * NP2)
                    sp.dma_start(batch(out), x[:]).then_inc(s["x_out"], 16)
                    sp.wait_ge(s["x_out"], 16)

                @block.gpsimd
                def _(pool):
                    ln_pool(0)
                    ffn_pool(0, 0)
                    ln_pool(1)
                    lin_pool()
                    ln_pool(2)
                    ffn_pool(1, 2)
                    ln_pool(3)
                    exp_pool(0)
                    ln_pool(4)
                    sm_pool()
                    ln_pool(5)
                    exp_pool(1)

                @block.scalar
                def _(act):
                    ln_act(0)
                    ffn_act(0, 0)
                    ln_act(1)
                    lin_act()
                    ln_act(2)
                    ffn_act(1, 2)
                    ln_act(3)
                    exp_act(0, 3)
                    ln_act(4)
                    sm_act()
                    ln_act(5)
                    exp_act(1, 5)

                @block.vector
                def _(dve):
                    ln_dve(0)
                    ffn_dve(0, 0, 0)
                    ln_dve(1)
                    lin_dve()
                    ln_dve(2)
                    ffn_dve(1, 2, 2)
                    ln_dve(3)
                    exp_dve(0, 3, 3)
                    ln_dve(4)
                    sm_dve()
                    ln_dve(5)
                    exp_dve(1, 5, 5)

                @block.tensor
                def _(pe):
                    ln_pe(0)
                    ffn_pe(0, 0)
                    ln_pe(1)
                    lin_pe()
                    ln_pe(2)
                    ffn_pe(1, 2)
                    ln_pe(3)
                    exp_pe(0, 3)
                    ln_pe(4)
                    sm_pe()
                    ln_pe(5)
                    exp_pe(1, 5)

            for v in s.values():
                nc.gpsimd.sem_clear(v)
            nc.all_engine_barrier()


_INS = (["L0_attn_x", "L0_attn_W_qkv", "L0_attn_W_o", "L0_ffn_W_r", "L0_ffn_W_k", "L0_ffn_W_v", "L0_ffn_mu_r",
         "L0_ffn_mu_k", "L1_attn_Wq", "L1_attn_Wk", "L1_attn_Wv", "L1_attn_Wo", "L1_ffn_W", "L1_ffn_Wp", "L1_ffn_bp",
         "L1_ffn_sim", "L1_ffn_temp"] + [f"L1_ffn_W{k}{e}" for e in range(NE) for k in "du"])


def kernel(**inputs):
    import concourse.bacc as _bacc
    from concourse.bass_utils import run_bass_kernel_spmd as _run

    nc = _bacc.Bacc("TRN2", target_bir_lowering=False, num_devices=1)
    arrays, aps = {}, {}
    for name in _INS:
        arr = np.ascontiguousarray(inputs[name])
        arrays[f"in_{name}"] = arr
        aps[name] = nc.dram_tensor(f"in_{name}", arr.shape, mybir.dt.from_np(arr.dtype), kind="ExternalInput").ap()
    out = nc.dram_tensor("out_0", (B, T, D), F32, kind="ExternalOutput").ap()
    macaron(nc, aps, out)
    r = _run(nc, [arrays], core_ids=[0])
    return r.results[0]["out_0"]
```

```python
import math
from contextlib import ExitStack

import numpy as np

import concourse.bass as bass
from concourse import mybir

F32 = mybir.dt.float32
F32R = mybir.dt.float32r
I32 = mybir.dt.int32
BF16 = mybir.dt.bfloat16
ALU = mybir.AluOpType
ACT = mybir.ActivationFunctionType
AX = mybir.AxisListType.X

P = 128
B, T, D = 8, 1024, 256
NB = B
H, DK = 16, 16
NT = T // P
KT = D // P
NP2 = NT // 2
CH = 512
NC = T // CH
G = 4
NG = H // G
HP = 32
PROJ = 64
RANKS = (1, 2, 4, 8)
NR = sum(RANKS)
NE = len(RANKS)
RW = PROJ + NR + NE
RS = 96
EPS = 1e-5
MASKED = -1e30
PAD = 8
TERMS = 4
MROW = TERMS * DK


def rope_table():
    inv = (1.0 / np.float32(10000.0) ** (np.arange(0, DK, 2, dtype=np.float32) / np.float32(DK))).astype(np.float32)
    freqs = np.outer(np.arange(T, dtype=np.float32), inv).astype(np.float32)
    emb = np.concatenate([freqs, freqs], -1)
    cos, sin = np.cos(emb), np.sin(emb)
    return np.stack([cos[:, 0::2].T, cos[:, 1::2].T, -sin[:, 0::2].T, sin[:, 1::2].T], axis=1).astype(np.float32)


def macaron(nc, a, out):
    ctx = ExitStack()
    with ctx:
        def sb(name, shape, dt=F32):
            return ctx.enter_context(nc.sbuf_tensor(name, shape, dt))

        def sem(name):
            return ctx.enter_context(nc.semaphore(name))

        wr0, wk0, wv0, wq1, wk1, wv1, wf1 = (
            sb(n, [P, KT, D]) for n in ("wr0", "wk0", "wv0", "wq1", "wk1", "wv1", "wf1"))
        wqkv = sb("wqkv", [P, KT, 3 * D])
        wo0 = sb("wo0", [P, NG, D])
        wo1 = sb("wo1", [P, KT, D])
        wroute = sb("wroute", [P, KT, RW])
        wup = sb("wup", [P, D])
        mu = sb("mu", [P, 2, 2, KT])
        bpb = sb("bpb", [P, PROJ])
        bsb = sb("bsb", [P, NE])
        first = sb("first", [P, NE])
        ident = sb("ident", [P, P])
        identb = sb("identb", [P, P], BF16)
        maskneg = sb("maskneg", [P, P], BF16)
        mask01 = sb("mask01", [P, P])
        hmask = sb("hmask", [P, H // KT])
        smask = sb("smask", [P, H // KT, HP])
        zcol = sb("zcol", [P, 1])
        x = sb("x", [P, NT, D])
        xnT = sb("xnT", [P, KT, PAD + T])
        vpad = sb("vpad", [P, NT, H, HP])
        stq = [sb(f"stq{i}", [P, G, T], F32R) for i in range(2)]
        stk = [sb(f"stk{i}", [P, G, T], F32R) for i in range(2)]
        stats = sb("stats", [P, NT, 6])
        mv = sb("mv", [P, NT, 2])
        varep = sb("varep", [P, NT])
        rstd = sb("rstd", [P, NT])
        ntmp = sb("ntmp", [P, 2 * H])
        small = sb("small", [P, 16, NT * NE])
        mhalf = sb("mhalf", [P, NE])
        mxa = sb("mxa", [P, 2, G * NT])
        mxb = sb("mxb", [P, 2, G * NT // 2])
        mhi = sb("mhi", [G * NT, 2, P], F32R)
        mlo = sb("mlo", [G * NT, 2, P], F32R)

        KB = 256
        arena = sb("arena", [P, 74 * KB])

        def ar(at, *shape):
            n = math.prod(shape)
            v = arena[:, at * KB:at * KB + n]
            names = "abcd"[:len(shape)]
            return v.rearrange(f"p ({' '.join(names)}) -> p {' '.join(names)}", **dict(zip(names[1:], shape[1:]))) if len(shape) > 1 else v

        xm = [ar(0, KT, T), ar(8, KT, T)]
        kact = ar(16, KT, T)
        th = ar(24, NT, D)
        prod = ar(32, 2, 2, D)
        xns = [ar(at, NT, D) for at in (64, 64, 40, 64, 64, 32)]
        qT = ar(0, KT, T)
        khT = ar(8, KT, T)
        kh = ar(16, NT, D)
        qbd = ar(24, 2, H, P)
        scm = ar(40, G, CH)
        ksq = ar(48, 2, 2, D)
        ssb = ar(52, 2, NG, P)
        yT = ar(56, NG, T)
        kvar = ar(72, 2, 2, H)
        krs = ar(73, 2, 2, H)
        ropet = ar(0, 4, T)
        pexp = ar(16, 4, 2, CH)
        rhi = ar(32, 2, 2, CH)
        rlo = ar(40, 2, 2, CH)
        ra = ar(48, 2, 2, CH)
        rb = ar(56, 2, 2, CH)
        ytok = ar(64, NT, D)
        yT1 = ar(0, KT, T)
        ypv = ar(8, 2, CH)
        yrec = ar(12, NC, G, G)
        projb = ar(0, NT, PROJ)
        psq = ar(2, NT, PROJ)
        dg = ar(4, NT, HP)
        dgT = ar(5, NT, P)
        raw = ar(0, 8, KT, D)
        rawp = ar(18, D)
        rawd = ar(19, D)
        rawu = ar(20, KT, 4, HP)
        rsim = ar(22, 16, NE)
        rbp = ar(23, P)
        kmean = ar(24, KT, H)
        ones = ar(25, P)

        bank = [ctx.enter_context(nc.psum_tensor(f"bank{i}", [P, 2 * CH], F32)) for i in range(4)]

        def ps(i, n=1):
            return bank[i // 2][:, (i % 2) * CH:(i % 2) * CH + n * CH]

        mm = nc.tensor.matmul

        w_in, w_mem, w_pool, w_norm = sem("w_in"), sem("w_mem"), sem("w_pool"), sem("w_norm")
        w_tr, w_cp, w_dve, w_act, w_ps2 = sem("w_tr"), sem("w_cp"), sem("w_dve"), sem("w_act"), sem("w_ps2")
        rope_d = nc.inline_tensor(rope_table(), name="rope_table").ap()
        q_d = nc.dram_tensor("q_halves", (2, 2, P, T), F32).ap()
        k_d = nc.dram_tensor("k_halves", (2, 2, P, T), F32).ap()
        zero_d = nc.inline_tensor(np.zeros((2, G * T), np.float32), name="zero_rows").ap()

        NLOAD = 8 + 1 + G + 1 + NE * 5 + 2 + 1 + 3

        with nc.allow_non_contiguous_dma(reason="small weights, once"), nc.Block() as block:
            @block.sync
            def _(sp):
                n = 0

                def load(dst, src):
                    nonlocal n
                    sp.dma_start(dst, src).then_inc(w_in, 16)
                    n += 1

                sp.wait_ge(w_mem, 3)
                for i, w in enumerate((a["L0_ffn_W_r"], a["L0_ffn_W_k"], a["L0_ffn_W_v"], a["L1_attn_Wq"], a["L1_attn_Wk"],
                                       a["L1_attn_Wv"], a["L1_ffn_W"], a["L1_attn_Wo"])):
                    load(raw[:, i], w.rearrange("(k p) c -> p k c", p=P))
                load(wqkv[:], a["L0_attn_W_qkv"].rearrange("(k p) c -> p k c", p=P))
                for j in range(G):
                    load(wo0[HP * j:HP * j + DK], a["L0_attn_W_o"].rearrange("(g j d) o -> j d g o", g=NG, j=G)[j])
                load(rawp[0:PROJ], a["L1_ffn_Wp"])
                r0 = 0
                for e, r in enumerate(RANKS):
                    load(rawd[r0:r0 + r], a[f"L1_ffn_Wd{e}"])
                    for j in range(4):
                        load(rawu[:, :, j, r0:r0 + r], a[f"L1_ffn_Wu{e}"].rearrange("(k p) r -> p k r", p=P))
                    r0 += r
                for m, w in enumerate((a["L0_ffn_mu_k"], a["L0_ffn_mu_r"])):
                    load(mu[:, m, 0, :], w.rearrange("(k p) -> p k", p=P))
                load(bpb[:], a["L1_ffn_bp"].partition_broadcast(P))
                load(rsim[0:PROJ, 0], a["L1_ffn_sim"])
                load(rsim[0:PROJ, 1, 0:1], a["L1_ffn_temp"].partition_broadcast(PROJ))
                load(rsim[0:PROJ, 2, 0:1], a["L1_ffn_bp"].rearrange("(p o) -> p o", o=1))
                assert n == NLOAD, n

            @block.gpsimd
            def _(pool):
                nc.gpsimd.memset(wo0[:], 0.0).then_inc(w_mem, 1)
                nc.gpsimd.memset(rawu[:], 0.0).then_inc(w_mem, 1)
                nc.gpsimd.memset(rawd[:], 0.0).then_inc(w_mem, 1)
                for t, v in ((ident, 0.0), (identb, 0.0), (maskneg, 0.0), (mask01, 1.0), (hmask, 1.0), (smask, 0.0),
                             (ones, 1.0)):
                    nc.gpsimd.memset(t[:], v).then_inc(w_pool, 1)
                nc.gpsimd.memset(xnT[:, :, 0:PAD], 0.0)
                nc.gpsimd.memset(zcol[:], 0.0)
                nc.gpsimd.memset(vpad[:], 1.0)
                nc.gpsimd.memset(mhalf[:], -0.5)
                for e in range(NE):
                    nc.gpsimd.memset(first[:, e:e + 1], float(NE - e))
                pool.wait_ge(w_pool, 7)
                nc.gpsimd.memset(smask[:, :, 0:DK], 1.0).then_inc(w_pool, 1)

                def select(t, op, fill, base, pattern, cm):
                    return nc.gpsimd.affine_select(out=t, in_=t, compare_op=op, fill=fill, base=base,
                                                   pattern=pattern, channel_multiplier=cm)

                select(ident[:], ALU.not_equal, 1.0, 0, [[-1, P]], 1).then_inc(w_pool, 1)
                select(identb[:], ALU.not_equal, 1.0, 0, [[-1, P]], 1).then_inc(w_pool, 1)
                select(maskneg[:], ALU.is_ge, MASKED, 0, [[-1, P]], 1).then_inc(w_pool, 1)
                select(mask01[:], ALU.is_ge, 0.0, 0, [[1, P]], -1).then_inc(w_pool, 1)
                pool.wait_ge(w_pool, 8)
                for t, pat in ((hmask[:], [[-DK, H // KT]]), (smask[:], [[-DK, H // KT], [0, HP]])):
                    neg = [[-s, c] for s, c in pat]
                    select(t, ALU.is_ge, 0.0, 0, pat, 1).then_inc(w_pool, 1)
                    pool.wait_ge(w_pool, 13 if t is not None and len(pat) == 1 else 15)
                    select(t, ALU.is_ge, 0.0, DK - 1, neg, -1).then_inc(w_pool, 1)
                pool.wait_ge(w_dve, 4)
                nc.gpsimd.tensor_scalar(rsim[0:PROJ, 5], rsim[0:PROJ, 5], 1e-24, None, ALU.max).then_inc(w_norm, 1)
                pool.wait_ge(w_norm, 1)
                nc.gpsimd.tensor_tensor(rsim[0:PROJ, 5], rsim[0:PROJ, 5], mhalf[0:PROJ, 0:NE], ALU.pow).then_inc(w_norm, 1)

            @block.tensor
            def _(pe):
                pe.wait_ge(w_in, 16 * NLOAD)
                pe.wait_ge(w_pool, 9)
                for m in range(7):
                    for k in range(KT):
                        for o in range(KT):
                            src = raw[:, m, o, k * P:(k + 1) * P]
                            last = nc.tensor.transpose(ps(m)[:, k * D + o * P:k * D + (o + 1) * P], src, ident[:])
                    last.then_inc(w_tr, 1)
                for k in range(KT):
                    nc.tensor.transpose(ps(7)[:, k * PROJ:(k + 1) * PROJ], rawp[0:PROJ, k * P:(k + 1) * P],
                                        ident[0:PROJ, 0:PROJ])
                    nc.tensor.transpose(ps(7)[:, 128 + 16 * k:144 + 16 * k], rawd[0:16, k * P:(k + 1) * P],
                                        ident[0:16, 0:16])
                    last = nc.tensor.transpose(ps(7)[:, 160 + k * P:160 + (k + 1) * P],
                                               rawu[:, k].rearrange("p j r -> p (j r)"), ident[:])
                last.then_inc(w_tr, 1)
                pe.wait_ge(w_cp, 2)
                for k in range(KT):
                    for o in range(KT):
                        last = nc.tensor.transpose(ps(0)[:, k * D + o * P:k * D + (o + 1) * P], raw[:, 7, o, k * P:(k + 1) * P],
                                                   ident[:])
                last.then_inc(w_tr, 1)
                pe.wait_ge(w_dve, 3)
                pe.wait_ge(w_cp, 5)
                mm(ps(2)[0:PROJ, 0:NE], ones[0:PROJ, 0:PROJ], rsim[0:PROJ, 3], start=True, stop=True).then_inc(w_ps2, 1)
                pe.wait_ge(w_dve, 7)
                for k in range(KT):
                    mm(ps(3)[:, 8 * k:8 * k + NE], rawp[0:PROJ, k * P:(k + 1) * P], rsim[0:PROJ, 6], start=True, stop=True)
                mm(ps(4)[:, 0:NE], rbp[0:PROJ, :], rsim[0:PROJ, 6], start=True, stop=True).then_inc(w_ps2, 1)

            @block.scalar
            def _(act):
                act.wait_ge(w_dve, 2)
                nc.scalar.activation(rsim[0:PROJ, 4, 0:1], rsim[0:PROJ, 4, 1:2], ACT.Exp).then_inc(w_act, 1)

            @block.vector
            def _(dve):
                dve.wait_ge(w_in, 16 * NLOAD)
                nc.vector.tensor_scalar(mu[:, :, 1, :], mu[:, :, 0, :], -1.0, 1.0, ALU.mult, ALU.add).then_inc(w_dve, 1)
                nc.vector.tensor_scalar(rsim[0:PROJ, 4, 1:2], rsim[0:PROJ, 1, 0:1], math.log(1.0 / 0.01), None,
                                        ALU.min).then_inc(w_dve, 1)
                nc.vector.tensor_tensor(rsim[0:PROJ, 3], rsim[0:PROJ, 0], rsim[0:PROJ, 0], ALU.mult).then_inc(w_dve, 1)
                for m, w in enumerate((wr0, wk0, wv0, wq1, wk1, wv1, wf1)):
                    dve.wait_ge(w_tr, m + 1)
                    if m in (3, 4):
                        for k in range(KT):
                            last = nc.vector.tensor_copy(w[:, k].rearrange("p (o i h) -> p o i h", o=2, i=DK // 2),
                                                         ps(m)[:, k * D:(k + 1) * D].rearrange("p (h i o) -> p o i h", o=2, i=DK // 2))
                        last.then_inc(w_cp, 1)
                    else:
                        nc.vector.tensor_copy(w[:].rearrange("p k c -> p (k c)"), ps(m)).then_inc(w_cp, 1)
                dve.wait_ge(w_tr, 8)
                nc.vector.tensor_copy(wroute[:, :, 0:PROJ], ps(7)[:, 0:128].rearrange("p (k c) -> p k c", k=KT))
                nc.vector.tensor_copy(wroute[:, :, PROJ:PROJ + NR], ps(7)[:, 128:160].rearrange("p (k c) -> p k c", k=KT)[:, :, 0:NR])
                nc.vector.tensor_copy(wup[:], ps(7)[:, 160:160 + D])
                dve.wait_ge(w_tr, 9)
                nc.vector.tensor_copy(wo1[:].rearrange("p k c -> p (k c)"), ps(0))
                dve.wait_ge(w_ps2, 1)
                nc.vector.tensor_copy(rsim[0:PROJ, 5], ps(2)[0:PROJ, 0:NE]).then_inc(w_dve, 1)
                dve.wait_ge(w_act, 1)
                dve.wait_ge(w_norm, 2)
                nc.vector.scalar_tensor_tensor(out=rsim[0:PROJ, 7], in0=rsim[0:PROJ, 0], scalar=rsim[0:PROJ, 4, 0:1],
                                               in1=rsim[0:PROJ, 5], op0=ALU.mult, op1=ALU.mult).then_inc(w_dve, 1)
                dve.wait_ge(w_dve, 5)
                nc.vector.tensor_copy(rsim[0:PROJ, 6], rsim[0:PROJ, 7]).then_inc(w_dve, 1)
                dve.wait_ge(w_pool, 7)
                nc.vector.tensor_scalar(rbp[0:PROJ, :], ones[0:PROJ, :], rsim[0:PROJ, 2, 0:1], None, ALU.mult).then_inc(w_dve, 1)
                dve.wait_ge(w_ps2, 2)
                nc.vector.tensor_copy(wroute[:, :, PROJ + NR:RW], ps(3)[:, 0:16].rearrange("p (k c) -> p k c", k=KT)[:, :, 0:NE])
                nc.vector.tensor_copy(bsb[:], ps(4)[:, 0:NE])
                wk = wqkv[:, :, D:2 * D].rearrange("p k (h d) -> p k h d", h=H)
                for k in range(KT):
                    nc.vector.reduce_sum(kmean[:, k], wk[:, k], AX).then_inc(w_dve, 1)
                dve.wait_ge(w_dve, 9)
                for k in range(KT):
                    nc.vector.scalar_tensor_tensor(out=wk[:, k], in0=kmean[:, k].unsqueeze(2).broadcast_to([P, H, DK]),
                                                   scalar=-1.0 / DK, in1=wk[:, k], op0=ALU.mult, op1=ALU.add)
                for s in (*stq, *stk):
                    nc.vector.memset(s[MROW:P].bitcast(F32), 0.0).then_inc(w_dve, 1)
                dve.wait_ge(w_dve, 13)
                for s in stk:
                    nc.vector.memset(s[MROW:MROW + 2].bitcast(F32), 1.0)

        names = ("x_in0 x_in1 x_out ln_stats ln_aggr ln_vareps newton xn_done xT_ps xT mix_t mix kT_ps relu_done kact_done r_ps th_done o_ps "
                 "prod_done x_upd q_ps qT_done qbd_done kv_ps ksq_done v_done kvar_done kvar_eps kh_done khT_ps khT_done "
                 "sc_ps sc_masked y_ps yT_done st_ps state_done oproj_ps rt_ps rt_step rt_act dgT_ps dgT_done base_ps "
                 "rope_in qk_ps rope_ab rope_r rope_hi rope_lo halves0 halves1 stack0 stack1 v1_ps v1_done s_ps smax_done mx_comb mT_ps "
                 "m_hl mrow0 mrow1 t_ps exp_done causal_done pv_done ypv_done yt_ps y_rec y_norm yT1_ps yT1_done").split()
        s = {n: sem(n) for n in names}
        stack_in = [s["stack0"], s["stack1"]]
        max_in = [s["mrow0"], s["mrow1"]]
        halves_out = [s["halves0"], s["halves1"]]
        x_in = [s["x_in0"], s["x_in1"]]

        with nc.Fori(0, NB) as it:
            with nc.Block() as block:
                nsteps = [0]

                def rsqrt(y, v, tmp):
                    def then(ins):
                        nsteps[0] += 1
                        ins.then_inc(s["newton"], 1)
                        nc.vector.wait_ge(s["newton"], nsteps[0])

                    then(nc.vector.tensor_scalar(tmp.bitcast(I32), v.bitcast(I32), 1, None, ALU.logical_shift_right))
                    then(nc.vector.tensor_scalar(y.bitcast(I32), tmp.bitcast(I32), -1.0, float(0x5f3759df), ALU.mult, ALU.add))
                    for _ in range(3):
                        then(nc.vector.scalar_tensor_tensor(out=tmp, in0=y, scalar=-0.5, in1=y, op0=ALU.mult, op1=ALU.mult))
                        then(nc.vector.tensor_tensor(tmp, tmp, v, ALU.mult))
                        then(nc.vector.scalar_tensor_tensor(out=y, in0=tmp, scalar=1.5, in1=y, op0=ALU.add, op1=ALU.mult))

                def ln_dve(n, c):
                    if n:
                        nc.vector.wait_ge(s["x_upd"], NP2 * (n - 1) + 2 * c + 2)
                    else:
                        nc.vector.wait_ge(x_in[c], 16)
                    ts = slice(4 * c, 4 * c + 4)
                    for t in range(4 * c, 4 * c + 4):
                        nc.vector.bn_stats(stats[:, t], x[:, t]).then_inc(s["ln_stats"], 1)
                    nc.vector.wait_ge(s["ln_stats"], NT * n + 4 * c + 4)
                    for t in range(4 * c, 4 * c + 4):
                        nc.vector.bn_aggr(mv[:, t], stats[:, t]).then_inc(s["ln_aggr"], 1)
                    nc.vector.wait_ge(s["ln_aggr"], NT * n + 4 * c + 4)
                    nc.vector.tensor_scalar(varep[:, ts], mv[:, ts, 1], EPS, None, ALU.add).then_inc(s["ln_vareps"], 1)
                    nc.vector.wait_ge(s["ln_vareps"], NC * n + c + 1)
                    rsqrt(rstd[:, ts], varep[:, ts], ntmp[:, 0:4])
                    for t in range(4 * c, 4 * c + 4):
                        nc.vector.tensor_scalar(xns[n][:, t], x[:, t], mv[:, t, 0:1], rstd[:, t:t + 1], ALU.subtract,
                                                ALU.mult).then_inc(s["xn_done"], 1)

                def ln_pe(n, c):
                    for t in range(4 * c, 4 * c + 4):
                        nc.tensor.wait_ge(s["xn_done"], NT * n + t + 1)
                        for k in range(KT):
                            last = nc.tensor.transpose(ps(2 * c + k)[:, (t % 4) * P:(t % 4 + 1) * P],
                                                       xns[n][:, t, k * P:(k + 1) * P], ident[:])
                            if t % 4 == 3:
                                last.then_inc(s["xT_ps"], 1)

                def ln_act(n, c):
                    for k in range(KT):
                        nc.scalar.wait_ge(s["xT_ps"], 4 * n + 2 * c + k + 1)
                        nc.scalar.copy(xnT[:, k, PAD + CH * c:PAD + CH * (c + 1)], ps(2 * c + k)).then_inc(s["xT"], 1)

                def xT_ready(eng, n, c=NC - 1):
                    eng.wait_ge(s["xT"], 4 * n + 2 * c + 2)

                def tok(t):
                    return slice(PAD + t * P, PAD + (t + 1) * P)

                def ffn_pool(f, n):
                    for c in range(NC):
                        xT_ready(nc.gpsimd, n, c)
                        for m in range(2):
                            for k in range(KT):
                                nc.gpsimd.tensor_scalar(xm[m][:, k, c * CH:(c + 1) * CH],
                                                        xnT[:, k, PAD - 1 + c * CH:PAD - 1 + (c + 1) * CH], mu[:, m, 1, k:k + 1],
                                                        zcol[:], ALU.mult, ALU.add).then_inc(s["mix_t"], 1)

                def ffn_dve(f, n):
                    for c in range(NC):
                        for m in range(2):
                            for k in range(KT):
                                nc.vector.wait_ge(s["mix_t"], 8 * f + 4 * c + 2 * m + k + 1)
                                nc.vector.scalar_tensor_tensor(out=xm[m][:, k, c * CH:(c + 1) * CH],
                                                               in0=xnT[:, k, PAD + c * CH:PAD + (c + 1) * CH],
                                                               scalar=mu[:, m, 0, k:k + 1], in1=xm[m][:, k, c * CH:(c + 1) * CH],
                                                               op0=ALU.mult, op1=ALU.add).then_inc(s["mix"], 1)
                    for p in range(NP2):
                        nc.vector.wait_ge(s["th_done"], NP2 * f + p + 1)
                        nc.vector.wait_ge(s["o_ps"], NP2 * f + p + 1)
                        nc.vector.scalar_tensor_tensor(out=prod[:, p % 2].rearrange("p t c -> p (t c)"),
                                                       in0=th[:, 2 * p:2 * p + 2].rearrange("p t c -> p (t c)"), scalar=1.0, in1=ps(4 + p),
                                                       op0=ALU.add, op1=ALU.mult).then_inc(s["prod_done"], 1)
                        nc.vector.wait_ge(s["prod_done"], NP2 * f + p + 1)
                        xv = x[:, 2 * p:2 * p + 2]
                        nc.vector.scalar_tensor_tensor(out=xv, in0=prod[:, p % 2], scalar=0.25, in1=xv, op0=ALU.mult,
                                                       op1=ALU.add).then_inc(s["x_upd"], 1)
                        if p % 2:
                            ln_dve(n + 1, p // 2)

                def ffn_pe(f, n):
                    for c in range(NC):
                        ln_pe(n, c)
                        nc.tensor.wait_ge(s["mix"], 8 * f + 4 * c + 2)
                        for m in range(KT):
                            for k in range(KT):
                                last = mm(ps(4 + 2 * c + m), wk0[:, k, m * P:(m + 1) * P], xm[0][:, k, c * CH:(c + 1) * CH],
                                          start=k == 0, stop=k == KT - 1)
                            last.then_inc(s["kT_ps"], 1)
                        nc.tensor.wait_ge(s["mix"], 8 * f + 4 * c + 4)
                        for p in (2 * c, 2 * c + 1):
                            for i in range(2):
                                for k in range(KT):
                                    last = mm(ps(p)[:, i * D:(i + 1) * D], xm[1][:, k, (2 * p + i) * P:(2 * p + i + 1) * P], wr0[:, k],
                                              start=k == 0, stop=k == KT - 1)
                            last.then_inc(s["r_ps"], 1)
                    for p in range(NP2):
                        nc.tensor.wait_ge(s["kact_done"], 4 * f + 2 * (p // 2) + 2)
                        for i in range(2):
                            for k in range(KT):
                                last = mm(ps(4 + p)[:, i * D:(i + 1) * D], kact[:, k, (2 * p + i) * P:(2 * p + i + 1) * P], wv0[:, k],
                                          start=k == 0, stop=k == KT - 1)
                        last.then_inc(s["o_ps"], 1)

                def ffn_act(f, n):
                    for c in range(NC):
                        ln_act(n, c)
                        for m in range(KT):
                            nc.scalar.wait_ge(s["kT_ps"], 4 * f + 2 * c + m + 1)
                            nc.scalar.activation(kact[:, m, c * CH:(c + 1) * CH], ps(4 + 2 * c + m), ACT.Relu).then_inc(s["relu_done"], 1)
                        for m in range(KT):
                            v = kact[:, m, c * CH:(c + 1) * CH]
                            nc.scalar.wait_ge(s["relu_done"], 4 * f + 2 * c + m + 1)
                            nc.scalar.activation(v, v, ACT.Square).then_inc(s["kact_done"], 1)
                        for p in (2 * c, 2 * c + 1):
                            nc.scalar.wait_ge(s["r_ps"], NP2 * f + p + 1)
                            nc.scalar.activation(th[:, 2 * p:2 * p + 2].rearrange("p t c -> p (t c)"), ps(p), ACT.Tanh,
                                                 scale=0.5).then_inc(s["th_done"], 1)

                def lin_pe():
                    for c in range(NC):
                        ln_pe(1, c)
                        xT_ready(nc.tensor, 1, c)
                        for m in range(KT):
                            for k in range(KT):
                                last = mm(ps(4 + 2 * c + m), wqkv[:, k, m * P:(m + 1) * P],
                                          xnT[:, k, PAD + c * CH:PAD + (c + 1) * CH], start=k == 0, stop=k == KT - 1)
                            last.then_inc(s["q_ps"], 1)
                    for p in range(NP2):
                        if p >= 2:
                            nc.tensor.wait_ge(s["kh_done"], p - 1)
                            nc.tensor.wait_ge(s["v_done"], p - 1)
                        for i in range(2):
                            for k in range(KT):
                                last = mm(ps(2 * (p % 2) + i), xnT[:, k, tok(2 * p + i)], wqkv[:, k, D:3 * D], start=k == 0,
                                          stop=k == KT - 1)
                        last.then_inc(s["kv_ps"], 1)
                    for t in range(NT):
                        nc.tensor.wait_ge(s["kh_done"], t // 2 + 1)
                        nc.tensor.wait_ge(s["qT_done"], 2 * (t // 4) + 2)
                        for k in range(KT):
                            last = nc.tensor.transpose(ps(4 + 2 * (t // 4) + k)[:, (t % 4) * P:(t % 4 + 1) * P],
                                                       kh[:, t, k * P:(k + 1) * P], ident[:])
                            if t % 4 == 3:
                                last.then_inc(s["khT_ps"], 1)
                    nc.tensor.wait_ge(s["v_done"], NP2)

                    def scores(t):
                        nc.tensor.wait_ge(s["khT_done"], 2 * (t // 4) + 2)
                        for g in range(NG):
                            u = NG * t + g
                            nc.tensor.wait_ge(s["qbd_done"], KT * t + g // 2 + 1)
                            if u >= 2:
                                nc.tensor.wait_ge(s["sc_masked"], u - 1)
                            mm(ps(u % 2), khT[:, g // 2, t * P:(t + 1) * P],
                               qbd[:, t % 2, G * g:G * g + G], start=True, stop=True).then_inc(s["sc_ps"], 1)

                    scores(0)
                    for t in range(NT):
                        if t < NT - 1:
                            if t:
                                nc.tensor.wait_ge(s["state_done"], t)
                            for g in range(NG):
                                last = mm(ps(4)[:, g * P:(g + 1) * P], kh[:, t, (g // 2) * P:(g // 2 + 1) * P],
                                          vpad[:, t, G * g:G * g + G], start=t == 0 and g == 0, stop=t == NT - 2,
                                          skip_group_check=True)
                            last.then_inc(s["st_ps"], 1)
                        y = ps(2 + t % 2)
                        if t >= 2:
                            nc.tensor.wait_ge(s["yT_done"], t - 1)
                        for g in range(NG):
                            if t:
                                nc.tensor.wait_ge(s["state_done"], t)
                                mm(y[:, g * P:(g + 1) * P], ssb[:, (t - 1) % 2, g], qT[:, g // 2, t * P:(t + 1) * P], start=True,
                                   stop=False, skip_group_check=True)
                            nc.tensor.wait_ge(s["sc_masked"], NG * t + g + 1)
                            for j in range(G):
                                last = mm(y[HP * j:HP * (j + 1), g * P:(g + 1) * P], vpad[:, t, G * g + j],
                                          scm[:, g, j * P:(j + 1) * P], start=t == 0, stop=True, skip_group_check=True,
                                          tile_position=(0, HP * j))
                        last.then_inc(s["y_ps"], 1)
                        if t < NT - 1:
                            scores(t + 1)
                    attn_out_pe(0, yT, wo0, NG, 4, lambda t: nc.tensor.wait_ge(s["yT_done"], t + 1))

                def attn_out_pe(n, yt, w, kn, b0, ready):
                    for p in range(NP2):
                        for i in range(2):
                            ready(2 * p + i)
                            for g in range(kn):
                                last = mm(ps(b0 + p)[:, i * D:(i + 1) * D], yt[:, g, (2 * p + i) * P:(2 * p + i + 1) * P], w[:, g],
                                          start=g == 0, stop=g == kn - 1)
                        last.then_inc(s["oproj_ps"], 1)

                def attn_out_dve(n, ln, b0):
                    for p in range(NP2):
                        nc.vector.wait_ge(s["oproj_ps"], NP2 * n + p + 1)
                        xv = x[:, 2 * p:2 * p + 2]
                        nc.vector.tensor_tensor(xv, xv, ps(b0 + p).rearrange("p (t c) -> p t c", t=2), ALU.add).then_inc(s["x_upd"], 1)
                        if p % 2:
                            ln_dve(ln, p // 2)

                def lin_act():
                    for c in range(NC):
                        ln_act(1, c)
                        for m in range(KT):
                            nc.scalar.wait_ge(s["q_ps"], 2 * c + m + 1)
                            nc.scalar.copy(qT[:, m, c * CH:(c + 1) * CH], ps(4 + 2 * c + m)).then_inc(s["qT_done"], 1)
                    for p in range(NP2):
                        nc.scalar.wait_ge(s["kv_ps"], p + 1)
                        if p >= 2:
                            nc.scalar.wait_ge(s["kvar_done"], p - 1)
                        kv = ps(2 * (p % 2), 2).rearrange("p (t c) -> p t c", t=2)
                        nc.scalar.copy(vpad[:, 2 * p:2 * p + 2, :, 0:DK],
                                       kv[:, :, D:2 * D].rearrange("p t (h d) -> p t h d", h=H)).then_inc(s["v_done"], 1)
                        nc.scalar.activation(ksq[:, p % 2], kv[:, :, 0:D], ACT.Square).then_inc(s["ksq_done"], 1)
                    for c in range(NC):
                        for k in range(KT):
                            nc.scalar.wait_ge(s["khT_ps"], 2 * c + k + 1)
                            nc.scalar.copy(khT[:, k, c * CH:(c + 1) * CH], ps(4 + 2 * c + k)).then_inc(s["khT_done"], 1)
                    for t in range(NT):
                        nc.scalar.wait_ge(s["y_ps"], t + 1)
                        nc.scalar.copy(yT[:, :, t * P:(t + 1) * P], ps(2 + t % 2).rearrange("p (g c) -> p g c", g=NG)).then_inc(s["yT_done"], 1)

                def lin_pool():
                    nc.gpsimd.wait_ge(s["x_upd"], NP2)
                    for t in range(NT):
                        nc.gpsimd.wait_ge(s["qT_done"], 2 * (t // 4) + 2)
                        if t >= 2:
                            nc.gpsimd.wait_ge(s["sc_ps"], NG * (t - 1))
                        for k in range(KT):
                            nc.gpsimd.tensor_tensor(qbd[:, t % 2, 8 * k:8 * k + 8], qT[:, k, t * P:(t + 1) * P].unsqueeze(1).broadcast_to([P, 8, P]),
                                                    hmask[:].unsqueeze(2).broadcast_to([P, 8, P]), ALU.mult).then_inc(s["qbd_done"], 1)

                def lin_dve():
                    for p in range(NP2):
                        nc.vector.wait_ge(s["ksq_done"], p + 1)
                        nc.vector.reduce_sum(kvar[:, p % 2].rearrange("p t h -> p (t h)"),
                                             ksq[:, p % 2].rearrange("p t (h d) -> p (t h) d", h=H), AX).then_inc(s["kvar_done"], 1)
                        nc.vector.wait_ge(s["kvar_done"], p + 1)
                        v = kvar[:, p % 2].rearrange("p t h -> p (t h)")
                        nc.vector.tensor_scalar(v, v, DK * EPS, None, ALU.add).then_inc(s["kvar_eps"], 1)
                        nc.vector.wait_ge(s["kvar_eps"], p + 1)
                        rsqrt(krs[:, p % 2].rearrange("p t h -> p (t h)"), v, ntmp[:])
                        for i in range(2):
                            last = nc.vector.scalar_tensor_tensor(
                                out=kh[:, 2 * p + i].rearrange("p (h d) -> p h d", h=H),
                                in0=ps(2 * (p % 2) + i)[:, 0:D].rearrange("p (h d) -> p h d", h=H), scalar=math.sqrt(DK),
                                in1=krs[:, p % 2, i].unsqueeze(2).broadcast_to([P, H, DK]), op0=ALU.mult, op1=ALU.mult)
                        last.then_inc(s["kh_done"], 1)
                    for t in range(NT):
                        for g in range(NG):
                            nc.vector.wait_ge(s["sc_ps"], NG * t + g + 1)
                            if t:
                                nc.vector.wait_ge(s["y_ps"], t)
                            nc.vector.tensor_tensor(scm[:, g].rearrange("p (j c) -> p j c", j=G),
                                                    ps((NG * t + g) % 2).rearrange("p (j c) -> p j c", j=G),
                                                    mask01[:].unsqueeze(1).broadcast_to([P, G, P]), ALU.mult).then_inc(s["sc_masked"], 1)
                        if t < NT - 1:
                            nc.vector.wait_ge(s["st_ps"], t + 1)
                            nc.vector.tensor_tensor(ssb[:, t % 2].rearrange("p (a b) c -> p a (b c)", a=2),
                                                    ps(4).rearrange("p (a c) -> p a c", a=2),
                                                    smask[:].rearrange("p h c -> p (h c)").unsqueeze(1).broadcast_to([P, 2, 2 * P]),
                                                    ALU.mult).then_inc(s["state_done"], 1)
                    attn_out_dve(0, 2, 4)

                def exp_pe(g, n):
                    for t in range(NT):
                        if t % 4 == 0:
                            ln_pe(n, t // 4)
                        xT_ready(nc.tensor, n, t // 4)
                        for k in range(KT):
                            last = mm(ps(4 + t // 4)[:, (t % 4) * RS:(t % 4) * RS + RW], xnT[:, k, tok(t)], wroute[:, k],
                                      start=k == 0, stop=k == KT - 1)
                        if t % 4 == 3:
                            last.then_inc(s["rt_ps"], 1)
                    for t in range(NT):
                        for k in range(KT):
                            mm(ps(t // 2)[:, (t % 2) * D:(t % 2 + 1) * D], xnT[:, k, tok(t)], wf1[:, k], start=k == 0 and t % 2 == 0,
                               stop=False, skip_group_check=True)
                    nc.tensor.wait_ge(s["rt_step"], RSTEPS * (g + 1))
                    for t in range(NT):
                        last = nc.tensor.transpose(ps(6, 2)[0:NR, t * P:(t + 1) * P], dg[:, t, 0:NR], ident[:])
                    last.then_inc(s["dgT_ps"], 1)
                    nc.tensor.wait_ge(s["dgT_done"], g + 1)
                    for t in range(NT):
                        last = mm(ps(t // 2)[:, (t % 2) * D:(t % 2 + 1) * D], dgT[0:NR, t], wup[0:NR], start=False, stop=True,
                                  skip_group_check=True)
                        if t % 2:
                            last.then_inc(s["base_ps"], 1)

                def exp_act(g, n):
                    for c in range(NC):
                        ln_act(n, c)
                    nc.scalar.wait_ge(s["rt_step"], RSTEPS * g + 1)
                    nc.scalar.activation(psq[:], projb[:], ACT.Square).then_inc(s["rt_act"], 1)
                    nc.scalar.wait_ge(s["rt_step"], RSTEPS * g + 7)
                    nc.scalar.activation(small[:, 4], small[:, 3], ACT.Exp).then_inc(s["rt_act"], 1)
                    nc.scalar.wait_ge(s["dgT_ps"], g + 1)
                    nc.scalar.copy(dgT[0:NR].rearrange("p q c -> p (q c)"), ps(6, 2)[0:NR, :]).then_inc(s["dgT_done"], 1)

                RSTEPS = 18

                def exp_dve(g, n):
                    step = [RSTEPS * g]

                    def then(ins, wait=True):
                        step[0] += 1
                        ins.then_inc(s["rt_step"], 1)
                        if wait:
                            nc.vector.wait_ge(s["rt_step"], step[0])

                    def row(i, shape=None):
                        return small[:, i].rearrange("p (t e) -> p t e", t=NT)

                    def one(i):
                        return small[:, i, 0:NT]

                    def over(v):
                        return v.unsqueeze(2).broadcast_to([P, NT, NE])

                    rt = ps(4, 2).rearrange("p (b c) -> p b c", b=2)[:, :, 0:4 * RS].rearrange("p b (t c) -> p b t c", t=4)
                    nc.vector.wait_ge(s["rt_ps"], 2 * g + 2)
                    for b in range(2):
                        last = nc.vector.tensor_tensor(projb[:, 4 * b:4 * b + 4], rt[:, b, :, 0:PROJ],
                                                       bpb[:].unsqueeze(1).broadcast_to([P, 4, PROJ]), ALU.add)
                    then(last, False)
                    for b in range(2):
                        last = nc.vector.tensor_tensor(row(0)[:, 4 * b:4 * b + 4], rt[:, b, :, PROJ + NR:RW],
                                                       bsb[:].unsqueeze(1).broadcast_to([P, 4, NE]), ALU.add)
                    then(last, False)
                    nc.vector.wait_ge(s["rt_act"], 2 * g + 1)
                    then(nc.vector.reduce_sum(one(1), psq[:], AX))
                    then(nc.vector.tensor_scalar(one(1), one(1), 1e-24, None, ALU.max))
                    rsqrt(one(11), one(1), one(12))
                    then(nc.vector.tensor_tensor(row(0), row(0), over(one(11)), ALU.mult))
                    then(nc.vector.reduce_max(one(2), row(0), AX))
                    then(nc.vector.tensor_tensor(row(3), row(0), over(one(2)), ALU.subtract))
                    then(nc.vector.tensor_scalar(row(5), row(3), 0.0, None, ALU.is_equal))
                    then(nc.vector.tensor_tensor(row(5), row(5), first[:].unsqueeze(1).broadcast_to([P, NT, NE]), ALU.mult))
                    then(nc.vector.reduce_max(one(6), row(5), AX))
                    then(nc.vector.tensor_tensor(row(7), row(5), over(one(6)), ALU.is_equal))
                    nc.vector.wait_ge(s["rt_act"], 2 * g + 2)
                    then(nc.vector.reduce_sum(one(8), row(4), AX))
                    then(nc.vector.reciprocal(one(9), one(8)))
                    then(nc.vector.tensor_tensor(row(10), row(7), over(one(9)), ALU.mult))
                    r0 = 0
                    for e, r in enumerate(RANKS):
                        for b in range(2):
                            last = nc.vector.tensor_tensor(dg[:, 4 * b:4 * b + 4, r0:r0 + r], rt[:, b, :, PROJ + r0:PROJ + r0 + r],
                                                           row(10)[:, 4 * b:4 * b + 4, e:e + 1].broadcast_to([P, 4, r]), ALU.mult)
                        then(last, False)
                        r0 += r
                    assert step[0] == RSTEPS * (g + 1)
                    for p in range(NP2):
                        nc.vector.wait_ge(s["base_ps"], NP2 * g + p + 1)
                        xv = x[:, 2 * p:2 * p + 2]
                        nc.vector.scalar_tensor_tensor(out=xv, in0=ps(p).rearrange("p (t c) -> p t c", t=2), scalar=0.5, in1=xv,
                                                       op0=ALU.mult, op1=ALU.add).then_inc(s["x_upd"], 1)
                        if g == 0 and p % 2:
                            ln_dve(n + 1, p // 2)

                ND = 6
                tunits = [(c, kb, hp) for c in range(NC) for kb in range(4 * (c + 1)) for hp in range(2)]
                NTU = len(tunits)
                sunits = [(h, qb, k0, min(P * (qb + 1), k0 + CH)) for h in range(G) for qb in range(NT)
                          for k0 in range(0, P * (qb + 1), CH)]
                NSU = len(sunits)
                PER = 3
                MT_AT = NSU // PER + 1
                DIAG = [u for u, (c, kb, hp) in enumerate(tunits) if kb >= 4 * c]

                def width(c, kb):
                    return CH - max(0, kb - 4 * c) * P

                def sm_sync():
                    sp = nc.sync
                    sp.wait_ge(s["x_upd"], 4 * NP2)
                    sp.dma_start(ropet[:].rearrange("p a t -> p (a t)"),
                                 rope_d.rearrange("i a t -> i (a t)").unsqueeze(1).broadcast_to([DK // 2, H, 4 * T])).then_inc(s["rope_in"], 16)
                    for u in range(2 * NC):
                        c, qk = u // 2, u % 2
                        cs = slice(c * CH, (c + 1) * CH)
                        dst = (q_d, k_d)[qk]
                        sp.wait_ge(s["rope_hi"], u + 1)
                        sp.dma_start(dst[0].rearrange("o r t -> r o t")[:, :, cs], rhi[:, u % 2]).then_inc(halves_out[u % 2], 16)
                        sp.wait_ge(s["rope_lo"], u + 1)
                        sp.dma_start(dst[1].rearrange("o r t -> r o t")[:, :, cs], rlo[:, u % 2]).then_inc(halves_out[u % 2], 16)
                    for i in range(2):
                        sp.wait_ge(halves_out[i], 16 * 2 * NC)
                    for g in range(NG):
                        b = g % 2
                        if g >= 2:
                            sp.wait_ge(s["t_ps"], NTU * (g - 1))
                            sp.wait_ge(max_in[b], 32 * (g // 2))
                        sp.dma_start(stq[b][MROW:MROW + 2].bitcast(F32).rearrange("p h t -> p (h t)"), zero_d).then_inc(stack_in[b], 16)

                        def rows(dram, half, n):
                            v = dram.rearrange("s o (i h) t -> (s o i) (h t)", h=H)
                            return v[DK * half:DK * (half + n), G * T * g:G * T * (g + 1)]

                        for st, r, src in ((stq[b], 0, rows(q_d, 0, 2)), (stq[b], 2, rows(q_d, 0, 2)), (stk[b], 0, rows(k_d, 0, 2)),
                                           (stk[b], 2, rows(k_d, 1, 1)), (stk[b], 3, rows(k_d, 0, 1))):
                            n = src.shape[0]
                            sp.dma_start(st[DK * r:DK * r + n].bitcast(F32).rearrange("p h t -> p (h t)"), src).then_inc(stack_in[b], 16)
                        if g >= 1:
                            max_rows(g - 1)
                    max_rows(NG - 1)

                def max_rows(g):
                    nc.sync.wait_ge(s["m_hl"], 2 * g + 2)
                    for i, m in enumerate((mhi, mlo)):
                        nc.sync.dma_start(stq[g % 2][MROW + i:MROW + i + 1].bitcast(F32).rearrange("o h t -> o (h t)"),
                                          m[:, g % 2].bitcast(F32)).then_inc(max_in[g % 2], 16)

                def sm_pe():
                    for c in range(NC):
                        ln_pe(4, c)
                        xT_ready(nc.tensor, 4, c)
                        for qk, w in enumerate((wq1, wk1)):
                            u = 2 * c + qk
                            if u >= 2:
                                nc.tensor.wait_ge(s["rope_ab"], 3 * (u - 1))
                            for m in range(KT):
                                for k in range(KT):
                                    last = mm(ps(4 + 2 * (u % 2) + m), w[:, k, m * P:(m + 1) * P], xnT[:, k, PAD + c * CH:PAD + (c + 1) * CH],
                                              start=k == 0, stop=k == KT - 1)
                            last.then_inc(s["qk_ps"], 1)
                    for p in range(NP2):
                        for i in range(2):
                            for k in range(KT):
                                last = mm(ps(p)[:, i * D:(i + 1) * D], xnT[:, k, tok(2 * p + i)], wv1[:, k], start=k == 0, stop=k == KT - 1)
                        last.then_inc(s["v1_ps"], 1)

                    def score(g, i):
                        h, qb, k0, k1 = sunits[i]
                        u = NSU * g + i
                        if i == 0:
                            nc.tensor.wait_ge(stack_in[g % 2], 16 * ND * (g // 2 + 1))
                        if u >= 2:
                            nc.tensor.wait_ge(s["smax_done"], u - 1)
                        diag = k1 == P * (qb + 1)
                        last = mm(ps(6 + u % 2)[:, 0:k1 - k0], stq[g % 2][:, h, qb * P:(qb + 1) * P], stk[g % 2][:, h, k0:k1],
                                  start=True, stop=not diag)
                        if diag:
                            last = mm(ps(6 + u % 2)[:, k1 - k0 - P:k1 - k0], identb[:], maskneg[:], start=False, stop=True)
                        last.then_inc(s["s_ps"], 1)

                    def max_transpose(g):
                        nc.tensor.wait_ge(s["mx_comb"], g + 1)
                        nc.tensor.transpose(ps(6)[0:G * NT, 0:P], mxa[:, g % 2], ident[:]).then_inc(s["mT_ps"], 1)

                    def tscore(g, i):
                        c, kb, hp = tunits[i]
                        u = NTU * g + i
                        if i == 0:
                            nc.tensor.wait_ge(max_in[g % 2], 32 * (g // 2 + 1))
                        if u >= 2:
                            nc.tensor.wait_ge(s["exp_done"], u - 1)
                        n = width(c, kb)
                        for j in range(2):
                            last = mm(ps(2 * (u % 2) + j)[:, 0:n], stk[g % 2][:, 2 * hp + j, kb * P:(kb + 1) * P],
                                      stq[g % 2][:, 2 * hp + j, (c + 1) * CH - n:(c + 1) * CH], start=True, stop=True)
                        last.then_inc(s["t_ps"], 1)

                    def values(g, i):
                        c, kb, hp = tunits[i]
                        u = NTU * g + i
                        yu = NC * g + c
                        n = width(c, kb)
                        nc.tensor.wait_ge(s["exp_done"], u + 1)
                        if i in DIAG:
                            nc.tensor.wait_ge(s["causal_done"], len(DIAG) * g + DIAG.index(i) + 1)
                        if kb == 0 and hp == 0 and yu >= 1:
                            nc.tensor.wait_ge(s["ypv_done"], yu)
                        for j in range(2):
                            q = HP * (2 * hp + j)
                            last = mm(ps(4)[q:q + HP, CH - n:CH], vpad[:, kb, G * g + 2 * hp + j], pexp[:, u % 4, j, 0:n],
                                      start=kb == 0, stop=kb == 4 * c + 3, tile_position=(0, q))
                        last.then_inc(s["pv_done"], 1)

                    def y_transpose(g, c):
                        yu = NC * g + c
                        nc.tensor.wait_ge(s["ypv_done"], yu + 1)
                        if yu:
                            nc.tensor.wait_ge(s["y_norm"], yu)
                        for b in range(4):
                            last = nc.tensor.transpose(ps(5)[:, b * P:(b + 1) * P], ypv[:, yu % 2, b * P:(b + 1) * P], ident[:])
                        last.then_inc(s["yt_ps"], 1)

                    for i in range(NSU):
                        score(0, i)
                    max_transpose(0)
                    nc.tensor.wait_ge(s["v1_done"], NP2)
                    for g in range(NG):
                        tscore(g, 0)
                        for i in range(NTU):
                            if i + 1 < NTU:
                                tscore(g, i + 1)
                            if g + 1 < NG:
                                for k in range(PER * i, min(PER * (i + 1), NSU)):
                                    score(g + 1, k)
                                if i == MT_AT:
                                    max_transpose(g + 1)
                            values(g, i)
                            if i == 9:
                                y_transpose(g, 0)
                            if i == 1 and g:
                                y_transpose(g - 1, 1)
                    y_transpose(NG - 1, 1)
                    nc.tensor.wait_ge(s["exp_done"], NTU * NG)
                    for c in range(NC):
                        nc.tensor.wait_ge(s["y_norm"], NC * (NG - 1) + c + 1)
                        for k in range(KT):
                            for b in range(4):
                                last = nc.tensor.transpose(ps(6 + k)[:, b * P:(b + 1) * P],
                                                           ytok[:, 4 * c + b, k * P:(k + 1) * P], ident[:])
                            last.then_inc(s["yT1_ps"], 1)
                        nc.tensor.wait_ge(s["yT1_done"], 2 * c + 2)
                    attn_out_pe(1, yT1, wo1, KT, 0, lambda t: None)

                def sm_dve():
                    nc.vector.wait_ge(s["rope_in"], 16)
                    for u in range(2 * NC):
                        c = u // 2
                        cs = slice(c * CH, (c + 1) * CH)
                        nc.vector.wait_ge(s["qk_ps"], u + 1)
                        if u >= 2:
                            nc.vector.wait_ge(s["rope_lo"], u - 1)
                        src = ps(4 + 2 * (u % 2), 2).rearrange("p (o c) -> p o c", o=2)
                        nc.vector.tensor_tensor(ra[:, u % 2], src, ropet[:, 0:2, cs], ALU.mult).then_inc(s["rope_ab"], 1)
                        for o in range(2):
                            nc.vector.tensor_tensor(rb[:, u % 2, o], src[:, 1 - o], ropet[:, 2 + o, cs], ALU.mult).then_inc(s["rope_ab"], 1)

                    def maxima(g, i):
                        h, qb, k0, k1 = sunits[i]
                        u = NSU * g + i
                        dst = mxa[:, g % 2, NT * h + qb:NT * h + qb + 1] if k0 == 0 else mxb[:, g % 2, 4 * h + qb - 4:4 * h + qb - 3]
                        nc.vector.wait_ge(s["s_ps"], u + 1)
                        nc.vector.reduce_max(dst, ps(6 + u % 2)[:, 0:k1 - k0], AX).then_inc(s["smax_done"], 1)

                    def negate(g):
                        nc.vector.wait_ge(s["smax_done"], NSU * (g + 1))
                        late = mxa[:, g % 2].rearrange("p (h q) -> p h q", h=G)[:, :, NT // 2:NT]
                        nc.vector.tensor_tensor(late, late, mxb[:, g % 2].rearrange("p (h q) -> p h q", h=G), ALU.max).then_inc(s["mx_comb"], 1)
                        nc.vector.wait_ge(s["mT_ps"], g + 1)
                        if g >= 2:
                            nc.vector.wait_ge(max_in[g % 2], 32 * (g // 2))
                        nc.vector.tensor_scalar(mhi[:, g % 2], ps(6)[0:G * NT, 0:P], -1.0, None, ALU.mult).then_inc(s["m_hl"], 1)
                        nc.vector.wait_ge(s["m_hl"], 2 * g + 1)
                        nc.vector.scalar_tensor_tensor(out=mlo[:, g % 2], in0=ps(6)[0:G * NT, 0:P], scalar=-1.0,
                                                       in1=mhi[:, g % 2].bitcast(F32), op0=ALU.mult, op1=ALU.subtract).then_inc(s["m_hl"], 1)

                    def finish(g, c):
                        yu = NC * g + c
                        yt = ps(5).rearrange("p (b j r) -> p b j r", b=4, j=G)
                        nc.vector.wait_ge(s["yt_ps"], yu + 1)
                        nc.vector.reciprocal(yrec[:, yu % 2], yt[:, :, :, DK]).then_inc(s["y_rec"], 1)
                        nc.vector.wait_ge(s["y_rec"], yu + 1)
                        nc.vector.tensor_tensor(ytok[:, 4 * c:4 * c + 4, G * DK * g:G * DK * (g + 1)].rearrange("p b (j d) -> p b j d", j=G),
                                                yt[:, :, :, 0:DK], yrec[:, yu % 2].unsqueeze(3).broadcast_to([P, 4, G, DK]),
                                                ALU.mult).then_inc(s["y_norm"], 1)

                    for i in range(NSU):
                        maxima(0, i)
                    negate(0)
                    for g in range(NG):
                        for i in range(NTU):
                            if g + 1 < NG:
                                for k in range(PER * i, min(PER * (i + 1), NSU)):
                                    maxima(g + 1, k)
                                if i == MT_AT:
                                    negate(g + 1)
                            if i == 9:
                                finish(g, 0)
                            if i == 1 and g:
                                finish(g - 1, 1)
                    finish(NG - 1, 1)
                    attn_out_dve(1, 5, 0)

                def sums_out(g, c):
                    nc.scalar.wait_ge(s["pv_done"], NTU * g + (8 if c == 0 else NTU))
                    if NC * g + c >= 2:
                        nc.scalar.wait_ge(s["yt_ps"], NC * g + c - 1)
                    nc.scalar.copy(ypv[:, c], ps(4)).then_inc(s["ypv_done"], 1)

                def sm_act():
                    for c in range(NC):
                        ln_act(4, c)
                    for u in range(2 * NC):
                        nc.scalar.wait_ge(s["rope_r"], u + 1)
                        if u >= 2:
                            nc.scalar.wait_ge(halves_out[u % 2], 32 * (u // 2))
                        nc.scalar.copy(rhi[:, u % 2].bitcast(F32R), ra[:, u % 2]).then_inc(s["rope_hi"], 1)
                    for p in range(NP2):
                        nc.scalar.wait_ge(s["v1_ps"], p + 1)
                        nc.scalar.copy(vpad[:, 2 * p:2 * p + 2, :, 0:DK],
                                       ps(p).rearrange("p (t h d) -> p t h d", t=2, h=H)).then_inc(s["v1_done"], 1)
                    for g in range(NG):
                        for i, (c, kb, hp) in enumerate(tunits):
                            u = NTU * g + i
                            n = width(c, kb)
                            nc.scalar.wait_ge(s["t_ps"], u + 1)
                            if u >= 4:
                                nc.scalar.wait_ge(s["pv_done"], u - 3)
                            nc.scalar.activation(pexp[:, u % 4, :, 0:n], ps(2 * (u % 2), 2).rearrange("p (j c) -> p j c", j=2)[:, :, 0:n],
                                                 ACT.Exp, scale=DK ** -0.5).then_inc(s["exp_done"], 1)
                            for at, gy, cy in ((8, g, 0), (0, g - 1, 1)):
                                if i == at and gy >= 0:
                                    sums_out(gy, cy)
                    sums_out(NG - 1, 1)
                    for c in range(NC):
                        for k in range(KT):
                            nc.scalar.wait_ge(s["yT1_ps"], 2 * c + k + 1)
                            nc.scalar.copy(yT1[:, k, c * CH:(c + 1) * CH], ps(6 + k)).then_inc(s["yT1_done"], 1)

                def sm_pool():
                    for u in range(2 * NC):
                        c, qk = u // 2, u % 2
                        nc.gpsimd.wait_ge(s["rope_ab"], 3 * (u + 1))
                        nc.gpsimd.tensor_tensor(ra[:, u % 2], ra[:, u % 2], rb[:, u % 2], ALU.add).then_inc(s["rope_r"], 1)
                        nc.gpsimd.wait_ge(s["rope_hi"], u + 1)
                        if u >= 2:
                            nc.gpsimd.wait_ge(halves_out[u % 2], 32 * (u // 2))
                        nc.gpsimd.tensor_tensor(rlo[:, u % 2].bitcast(F32R), ra[:, u % 2], rhi[:, u % 2], ALU.subtract).then_inc(s["rope_lo"], 1)
                    for g in range(NG):
                        for i in DIAG:
                            u = NTU * g + i
                            nc.gpsimd.wait_ge(s["exp_done"], u + 1)
                            v = pexp[:, u % 4, :, 0:P]
                            nc.gpsimd.affine_select(out=v, in_=v, compare_op=ALU.is_ge, fill=0.0, base=0, pattern=[[0, 2], [1, P]],
                                                    channel_multiplier=-1).then_inc(s["causal_done"], 1)

                def chunk(dram, c):
                    return dram.rearrange("b t c -> (b t) c")[bass.ds(it * T + c * CH, CH)].rearrange("(t p) c -> p t c", p=P)

                @block.sync
                def _(sp):
                    for c in range(NC):
                        sp.dma_start(x[:, 4 * c:4 * c + 4], chunk(a["L0_attn_x"], c)).then_inc(x_in[c], 16)
                    sm_sync()
                    for c in range(NC):
                        sp.wait_ge(s["x_upd"], 5 * NP2 + 2 * c + 2)
                        sp.dma_start(chunk(out, c), x[:, 4 * c:4 * c + 4]).then_inc(s["x_out"], 16)
                    sp.wait_ge(s["x_out"], 16 * NC)

                @block.gpsimd
                def _(pool):
                    ffn_pool(0, 0)
                    lin_pool()
                    ffn_pool(1, 2)
                    sm_pool()

                @block.scalar
                def _(act):
                    ffn_act(0, 0)
                    lin_act()
                    ffn_act(1, 2)
                    exp_act(0, 3)
                    sm_act()
                    exp_act(1, 5)

                @block.vector
                def _(dve):
                    for c in range(NC):
                        ln_dve(0, c)
                    ffn_dve(0, 0)
                    lin_dve()
                    ffn_dve(1, 2)
                    exp_dve(0, 3)
                    sm_dve()
                    exp_dve(1, 5)

                @block.tensor
                def _(pe):
                    ffn_pe(0, 0)
                    lin_pe()
                    ffn_pe(1, 2)
                    exp_pe(0, 3)
                    sm_pe()
                    exp_pe(1, 5)

            for v in s.values():
                nc.gpsimd.sem_clear(v)
            nc.all_engine_barrier()


_INS = (["L0_attn_x", "L0_attn_W_qkv", "L0_attn_W_o", "L0_ffn_W_r", "L0_ffn_W_k", "L0_ffn_W_v", "L0_ffn_mu_r",
         "L0_ffn_mu_k", "L1_attn_Wq", "L1_attn_Wk", "L1_attn_Wv", "L1_attn_Wo", "L1_ffn_W", "L1_ffn_Wp", "L1_ffn_bp",
         "L1_ffn_sim", "L1_ffn_temp"] + [f"L1_ffn_W{k}{e}" for e in range(NE) for k in "du"])


def kernel(**inputs):
    import concourse.bacc as _bacc
    from concourse.bass_utils import run_bass_kernel_spmd as _run

    nc = _bacc.Bacc("TRN2", target_bir_lowering=False, num_devices=1)
    arrays, aps = {}, {}
    for name in _INS:
        arr = np.ascontiguousarray(inputs[name])
        arrays[f"in_{name}"] = arr
        aps[name] = nc.dram_tensor(f"in_{name}", arr.shape, mybir.dt.from_np(arr.dtype), kind="ExternalInput").ap()
    out = nc.dram_tensor("out_0", (B, T, D), F32, kind="ExternalOutput").ap()
    macaron(nc, aps, out)
    r = _run(nc, [arrays], core_ids=[0])
    return r.results[0]["out_0"]
```

```python
import math
from contextlib import ExitStack

import numpy as np

import concourse.bass as bass
from concourse import mybir

F32 = mybir.dt.float32
F32R = mybir.dt.float32r
I32 = mybir.dt.int32
BF16 = mybir.dt.bfloat16
ALU = mybir.AluOpType
ACT = mybir.ActivationFunctionType
AX = mybir.AxisListType.X

P = 128
B, T, D = 8, 1024, 256
NB = B
H, DK = 16, 16
NT = T // P
KT = D // P
NP2 = NT // 2
CH = 512
NC = T // CH
G = 4
NG = H // G
HP = 32
PROJ = 64
RANKS = (1, 2, 4, 8)
NR = sum(RANKS)
NE = len(RANKS)
RW = PROJ + NR + NE
RS = 96
EPS = 1e-5
MASKED = -1e30
PAD = 8
TERMS = 4
NPX = 6
NST = 3
MROW = TERMS * DK


def rope_table():
    inv = (1.0 / np.float32(10000.0) ** (np.arange(0, DK, 2, dtype=np.float32) / np.float32(DK))).astype(np.float32)
    freqs = np.outer(np.arange(T, dtype=np.float32), inv).astype(np.float32)
    emb = np.concatenate([freqs, freqs], -1)
    cos, sin = np.cos(emb), np.sin(emb)
    return np.stack([cos[:, 0::2].T, cos[:, 1::2].T, -sin[:, 0::2].T, sin[:, 1::2].T], axis=1).astype(np.float32)


def macaron(nc, a, out):
    ctx = ExitStack()
    with ctx:
        def sb(name, shape, dt=F32):
            return ctx.enter_context(nc.sbuf_tensor(name, shape, dt))

        def sem(name):
            return ctx.enter_context(nc.semaphore(name))

        wr0, wk0, wv0, wq1, wk1, wv1, wf1 = (
            sb(n, [P, KT, D]) for n in ("wr0", "wk0", "wv0", "wq1", "wk1", "wv1", "wf1"))
        wqkv = sb("wqkv", [P, KT, 3 * D])
        wo0 = sb("wo0", [P, NG, D])
        wo1 = sb("wo1", [P, KT, D])
        wroute = sb("wroute", [P, KT, RW])
        wup = sb("wup", [P, D])
        mu = sb("mu", [P, 2, 2, KT])
        bpb = sb("bpb", [P, PROJ])
        bsb = sb("bsb", [P, NE])
        first = sb("first", [P, NE])
        ident = sb("ident", [P, P])
        identb = sb("identb", [P, P], BF16)
        maskneg = sb("maskneg", [P, P], BF16)
        mask01 = sb("mask01", [P, P])
        hmask = sb("hmask", [P, H // KT])
        smask = sb("smask", [P, H // KT, HP])
        zcol = sb("zcol", [P, 1])
        x = sb("x", [P, NT, D])
        xnT = sb("xnT", [P, KT, PAD + T])
        vpad = sb("vpad", [P, NT, H, HP])
        stq = [sb(f"stq{i}", [P, G, T], F32R)[:] for i in range(2)]
        stk = [sb(f"stk{i}", [P, G, T], F32R)[:] for i in range(2)]
        stats = sb("stats", [P, NT, 6])
        mv = sb("mv", [P, NT, 2])
        varep = sb("varep", [P, NT])
        rstd = sb("rstd", [P, NT])
        ntmp = sb("ntmp", [P, 2 * H])
        small = sb("small", [P, 16, NT * NE])
        mhalf = sb("mhalf", [P, NE])
        mxa = sb("mxa", [P, 2, G * NT])
        mxb = sb("mxb", [P, 2, G * NT // 2])
        mhi = sb("mhi", [G * NT, 2, P], F32R)
        mlo = sb("mlo", [G * NT, 2, P], F32R)

        KB = 256
        with nc.sbuf_tensor("arena", [P, 74 * KB], F32) as arena:
            pass
        sb("under_third", [P, 32 * KB])
        third = [sb(n, [P, G, T], F32R)[:] for n in ("stq2", "stk2")]
        sb("over_third", [P, 10 * KB])

        def ar(at, *shape):
            n = math.prod(shape)
            v = arena[:, at * KB:at * KB + n]
            names = "abcd"[:len(shape)]
            return v.rearrange(f"p ({' '.join(names)}) -> p {' '.join(names)}", **dict(zip(names[1:], shape[1:]))) if len(shape) > 1 else v

        xm = [ar(0, KT, T), ar(8, KT, T)]
        kact = ar(16, KT, T)
        th = ar(24, NT, D)
        prod = ar(32, 2, 2, D)
        xns = [ar(at, NT, D) for at in (64, 64, 40, 64, 64, 32)]
        qT = ar(0, KT, T)
        khT = ar(8, KT, T)
        kh = ar(16, NT, D)
        qbd = ar(24, 2, H, P)
        scm = ar(40, G, CH)
        ksq = ar(48, 2, 2, D)
        ssb = ar(52, 2, NG, P)
        yT = ar(56, NG, T)
        kvar = ar(72, 2, 2, H)
        krs = ar(73, 2, 2, H)
        ropet = ar(0, 4, T)
        pexp = ar(8, NPX, 2, CH)
        rhi = ar(32, 2, 2, CH)
        rlo = ar(40, 2, 2, CH)
        ra = ar(48, 2, 2, CH)
        rb = ar(56, 2, 2, CH)
        ytok = ar(64, NT, D)
        stq.append(third[0])
        stk.append(third[1])
        yT1 = ar(8, KT, T)
        ypv = ar(0, 2, CH)
        yrec = ar(4, NC, G, G)
        projb = ar(0, NT, PROJ)
        psq = ar(2, NT, PROJ)
        dg = ar(4, NT, HP)
        dgT = ar(5, NT, P)
        raw = ar(0, 8, KT, D)
        rawp = ar(18, D)
        rawd = ar(19, D)
        rawu = ar(20, KT, 4, HP)
        rsim = ar(22, 16, NE)
        rbp = ar(23, P)
        kmean = ar(24, KT, H)
        ones = ar(25, P)

        bank = [ctx.enter_context(nc.psum_tensor(f"bank{i}", [P, 2 * CH], F32)) for i in range(4)]

        def ps(i, n=1):
            return bank[i // 2][:, (i % 2) * CH:(i % 2) * CH + n * CH]

        mm = nc.tensor.matmul

        w_in, w_mem, w_pool, w_norm = sem("w_in"), sem("w_mem"), sem("w_pool"), sem("w_norm")
        w_tr, w_cp, w_dve, w_act, w_ps2 = sem("w_tr"), sem("w_cp"), sem("w_dve"), sem("w_act"), sem("w_ps2")
        rope_d = nc.inline_tensor(rope_table(), name="rope_table").ap()
        q_d = nc.dram_tensor("q_halves", (2, 2, P, T), F32).ap()
        k_d = nc.dram_tensor("k_halves", (2, 2, P, T), F32).ap()
        zero_d = nc.inline_tensor(np.zeros((2, G * T), np.float32), name="zero_rows").ap()

        NLOAD = 8 + 1 + G + 1 + NE * 5 + 2 + 1 + 3

        with nc.allow_non_contiguous_dma(reason="small weights, once"), nc.Block() as block:
            @block.sync
            def _(sp):
                n = 0

                def load(dst, src):
                    nonlocal n
                    sp.dma_start(dst, src).then_inc(w_in, 16)
                    n += 1

                sp.wait_ge(w_mem, 3)
                for i, w in enumerate((a["L0_ffn_W_r"], a["L0_ffn_W_k"], a["L0_ffn_W_v"], a["L1_attn_Wq"], a["L1_attn_Wk"],
                                       a["L1_attn_Wv"], a["L1_ffn_W"], a["L1_attn_Wo"])):
                    load(raw[:, i], w.rearrange("(k p) c -> p k c", p=P))
                load(wqkv[:], a["L0_attn_W_qkv"].rearrange("(k p) c -> p k c", p=P))
                for j in range(G):
                    load(wo0[HP * j:HP * j + DK], a["L0_attn_W_o"].rearrange("(g j d) o -> j d g o", g=NG, j=G)[j])
                load(rawp[0:PROJ], a["L1_ffn_Wp"])
                r0 = 0
                for e, r in enumerate(RANKS):
                    load(rawd[r0:r0 + r], a[f"L1_ffn_Wd{e}"])
                    for j in range(4):
                        load(rawu[:, :, j, r0:r0 + r], a[f"L1_ffn_Wu{e}"].rearrange("(k p) r -> p k r", p=P))
                    r0 += r
                for m, w in enumerate((a["L0_ffn_mu_k"], a["L0_ffn_mu_r"])):
                    load(mu[:, m, 0, :], w.rearrange("(k p) -> p k", p=P))
                load(bpb[:], a["L1_ffn_bp"].partition_broadcast(P))
                load(rsim[0:PROJ, 0], a["L1_ffn_sim"])
                load(rsim[0:PROJ, 1, 0:1], a["L1_ffn_temp"].partition_broadcast(PROJ))
                load(rsim[0:PROJ, 2, 0:1], a["L1_ffn_bp"].rearrange("(p o) -> p o", o=1))
                assert n == NLOAD, n

            @block.gpsimd
            def _(pool):
                nc.gpsimd.memset(wo0[:], 0.0).then_inc(w_mem, 1)
                nc.gpsimd.memset(rawu[:], 0.0).then_inc(w_mem, 1)
                nc.gpsimd.memset(rawd[:], 0.0).then_inc(w_mem, 1)
                for t, v in ((ident, 0.0), (identb, 0.0), (maskneg, 0.0), (mask01, 1.0), (hmask, 1.0), (smask, 0.0),
                             (ones, 1.0)):
                    nc.gpsimd.memset(t[:], v).then_inc(w_pool, 1)
                nc.gpsimd.memset(xnT[:, :, 0:PAD], 0.0)
                nc.gpsimd.memset(zcol[:], 0.0)
                nc.gpsimd.memset(vpad[:], 1.0)
                nc.gpsimd.memset(mhalf[:], -0.5)
                for e in range(NE):
                    nc.gpsimd.memset(first[:, e:e + 1], float(NE - e))
                pool.wait_ge(w_pool, 7)
                nc.gpsimd.memset(smask[:, :, 0:DK], 1.0).then_inc(w_pool, 1)

                def select(t, op, fill, base, pattern, cm):
                    return nc.gpsimd.affine_select(out=t, in_=t, compare_op=op, fill=fill, base=base,
                                                   pattern=pattern, channel_multiplier=cm)

                select(ident[:], ALU.not_equal, 1.0, 0, [[-1, P]], 1).then_inc(w_pool, 1)
                select(identb[:], ALU.not_equal, 1.0, 0, [[-1, P]], 1).then_inc(w_pool, 1)
                select(maskneg[:], ALU.is_ge, MASKED, 0, [[-1, P]], 1).then_inc(w_pool, 1)
                select(mask01[:], ALU.is_ge, 0.0, 0, [[1, P]], -1).then_inc(w_pool, 1)
                pool.wait_ge(w_pool, 8)
                for t, pat in ((hmask[:], [[-DK, H // KT]]), (smask[:], [[-DK, H // KT], [0, HP]])):
                    neg = [[-s, c] for s, c in pat]
                    select(t, ALU.is_ge, 0.0, 0, pat, 1).then_inc(w_pool, 1)
                    pool.wait_ge(w_pool, 13 if t is not None and len(pat) == 1 else 15)
                    select(t, ALU.is_ge, 0.0, DK - 1, neg, -1).then_inc(w_pool, 1)
                pool.wait_ge(w_dve, 4)
                nc.gpsimd.tensor_scalar(rsim[0:PROJ, 5], rsim[0:PROJ, 5], 1e-24, None, ALU.max).then_inc(w_norm, 1)
                pool.wait_ge(w_norm, 1)
                nc.gpsimd.tensor_tensor(rsim[0:PROJ, 5], rsim[0:PROJ, 5], mhalf[0:PROJ, 0:NE], ALU.pow).then_inc(w_norm, 1)

            @block.tensor
            def _(pe):
                pe.wait_ge(w_in, 16 * NLOAD)
                pe.wait_ge(w_pool, 9)
                for m in range(7):
                    for k in range(KT):
                        for o in range(KT):
                            src = raw[:, m, o, k * P:(k + 1) * P]
                            last = nc.tensor.transpose(ps(m)[:, k * D + o * P:k * D + (o + 1) * P], src, ident[:])
                    last.then_inc(w_tr, 1)
                for k in range(KT):
                    nc.tensor.transpose(ps(7)[:, k * PROJ:(k + 1) * PROJ], rawp[0:PROJ, k * P:(k + 1) * P],
                                        ident[0:PROJ, 0:PROJ])
                    nc.tensor.transpose(ps(7)[:, 128 + 16 * k:144 + 16 * k], rawd[0:16, k * P:(k + 1) * P],
                                        ident[0:16, 0:16])
                    last = nc.tensor.transpose(ps(7)[:, 160 + k * P:160 + (k + 1) * P],
                                               rawu[:, k].rearrange("p j r -> p (j r)"), ident[:])
                last.then_inc(w_tr, 1)
                pe.wait_ge(w_cp, 2)
                for k in range(KT):
                    for o in range(KT):
                        last = nc.tensor.transpose(ps(0)[:, k * D + o * P:k * D + (o + 1) * P], raw[:, 7, o, k * P:(k + 1) * P],
                                                   ident[:])
                last.then_inc(w_tr, 1)
                pe.wait_ge(w_dve, 3)
                pe.wait_ge(w_cp, 5)
                mm(ps(2)[0:PROJ, 0:NE], ones[0:PROJ, 0:PROJ], rsim[0:PROJ, 3], start=True, stop=True).then_inc(w_ps2, 1)
                pe.wait_ge(w_dve, 7)
                for k in range(KT):
                    mm(ps(3)[:, 8 * k:8 * k + NE], rawp[0:PROJ, k * P:(k + 1) * P], rsim[0:PROJ, 6], start=True, stop=True)
                mm(ps(4)[:, 0:NE], rbp[0:PROJ, :], rsim[0:PROJ, 6], start=True, stop=True).then_inc(w_ps2, 1)

            @block.scalar
            def _(act):
                act.wait_ge(w_dve, 2)
                nc.scalar.activation(rsim[0:PROJ, 4, 0:1], rsim[0:PROJ, 4, 1:2], ACT.Exp).then_inc(w_act, 1)

            @block.vector
            def _(dve):
                dve.wait_ge(w_in, 16 * NLOAD)
                nc.vector.tensor_scalar(mu[:, :, 1, :], mu[:, :, 0, :], -1.0, 1.0, ALU.mult, ALU.add).then_inc(w_dve, 1)
                nc.vector.tensor_scalar(rsim[0:PROJ, 4, 1:2], rsim[0:PROJ, 1, 0:1], math.log(1.0 / 0.01), None,
                                        ALU.min).then_inc(w_dve, 1)
                nc.vector.tensor_tensor(rsim[0:PROJ, 3], rsim[0:PROJ, 0], rsim[0:PROJ, 0], ALU.mult).then_inc(w_dve, 1)
                for m, w in enumerate((wr0, wk0, wv0, wq1, wk1, wv1, wf1)):
                    dve.wait_ge(w_tr, m + 1)
                    if m in (3, 4):
                        for k in range(KT):
                            last = nc.vector.tensor_copy(w[:, k].rearrange("p (o i h) -> p o i h", o=2, i=DK // 2),
                                                         ps(m)[:, k * D:(k + 1) * D].rearrange("p (h i o) -> p o i h", o=2, i=DK // 2))
                        last.then_inc(w_cp, 1)
                    else:
                        nc.vector.tensor_copy(w[:].rearrange("p k c -> p (k c)"), ps(m)).then_inc(w_cp, 1)
                dve.wait_ge(w_tr, 8)
                nc.vector.tensor_copy(wroute[:, :, 0:PROJ], ps(7)[:, 0:128].rearrange("p (k c) -> p k c", k=KT))
                nc.vector.tensor_copy(wroute[:, :, PROJ:PROJ + NR], ps(7)[:, 128:160].rearrange("p (k c) -> p k c", k=KT)[:, :, 0:NR])
                nc.vector.tensor_copy(wup[:], ps(7)[:, 160:160 + D])
                dve.wait_ge(w_tr, 9)
                nc.vector.tensor_copy(wo1[:].rearrange("p k c -> p (k c)"), ps(0))
                dve.wait_ge(w_ps2, 1)
                nc.vector.tensor_copy(rsim[0:PROJ, 5], ps(2)[0:PROJ, 0:NE]).then_inc(w_dve, 1)
                dve.wait_ge(w_act, 1)
                dve.wait_ge(w_norm, 2)
                nc.vector.scalar_tensor_tensor(out=rsim[0:PROJ, 7], in0=rsim[0:PROJ, 0], scalar=rsim[0:PROJ, 4, 0:1],
                                               in1=rsim[0:PROJ, 5], op0=ALU.mult, op1=ALU.mult).then_inc(w_dve, 1)
                dve.wait_ge(w_dve, 5)
                nc.vector.tensor_copy(rsim[0:PROJ, 6], rsim[0:PROJ, 7]).then_inc(w_dve, 1)
                dve.wait_ge(w_pool, 7)
                nc.vector.tensor_scalar(rbp[0:PROJ, :], ones[0:PROJ, :], rsim[0:PROJ, 2, 0:1], None, ALU.mult).then_inc(w_dve, 1)
                dve.wait_ge(w_ps2, 2)
                nc.vector.tensor_copy(wroute[:, :, PROJ + NR:RW], ps(3)[:, 0:16].rearrange("p (k c) -> p k c", k=KT)[:, :, 0:NE])
                nc.vector.tensor_copy(bsb[:], ps(4)[:, 0:NE])
                wk = wqkv[:, :, D:2 * D].rearrange("p k (h d) -> p k h d", h=H)
                for k in range(KT):
                    nc.vector.reduce_sum(kmean[:, k], wk[:, k], AX).then_inc(w_dve, 1)
                dve.wait_ge(w_dve, 9)
                for k in range(KT):
                    nc.vector.scalar_tensor_tensor(out=wk[:, k], in0=kmean[:, k].unsqueeze(2).broadcast_to([P, H, DK]),
                                                   scalar=-1.0 / DK, in1=wk[:, k], op0=ALU.mult, op1=ALU.add)
                for s in (*stq[:2], *stk[:2]):
                    nc.vector.memset(s[MROW:P].bitcast(F32), 0.0).then_inc(w_dve, 1)
                dve.wait_ge(w_dve, 13)
                for s in stk[:2]:
                    nc.vector.memset(s[MROW:MROW + 2].bitcast(F32), 1.0)

        names = ("x_in0 x_in1 x_out ln_stats ln_aggr ln_vareps newton xn_done xT_ps xT mix_k mix_r mix kT_ps relu_done kact_done r_ps th_done o_ps "
                 "prod_done x_upd q_ps qT_done qbd_done kv_ps ksq_done v_done kvar_done kvar_eps kh_done khT_ps khT_done "
                 "sc_ps sc_masked y_ps yT_done st_ps state_done oproj_ps rt_ps rt_step rt_act dgT_ps dgT_done base_ps "
                 "rope_in qk_ps rope_ab rope_r rope_hi rope_lo halves0 halves1 stack0 stack1 stack2 third_rows v1_ps v1_done ring_full ring_used mx_comb "
                 "m_hl mrow0 mrow1 mrow2 t_ps exp_done causal_done pv_done ypv_done y_rec yT1_ps yT1_done").split()
        s = {n: sem(n) for n in names}
        stack_in = [s[f"stack{i}"] for i in range(NST)]
        max_in = [s[f"mrow{i}"] for i in range(NST)]
        halves_out = [s["halves0"], s["halves1"]]
        x_in = [s["x_in0"], s["x_in1"]]

        with nc.Fori(0, NB) as it:
            with nc.Block() as block:
                nsteps = [0]

                def rsqrt(y, v, tmp):
                    def then(ins):
                        nsteps[0] += 1
                        ins.then_inc(s["newton"], 1)
                        nc.vector.wait_ge(s["newton"], nsteps[0])

                    then(nc.vector.tensor_scalar(tmp.bitcast(I32), v.bitcast(I32), 1, None, ALU.logical_shift_right))
                    then(nc.vector.tensor_scalar(y.bitcast(I32), tmp.bitcast(I32), -1.0, float(0x5f3759df), ALU.mult, ALU.add))
                    for _ in range(3):
                        then(nc.vector.scalar_tensor_tensor(out=tmp, in0=y, scalar=-0.5, in1=y, op0=ALU.mult, op1=ALU.mult))
                        then(nc.vector.tensor_tensor(tmp, tmp, v, ALU.mult))
                        then(nc.vector.scalar_tensor_tensor(out=y, in0=tmp, scalar=1.5, in1=y, op0=ALU.add, op1=ALU.mult))

                def ln_dve(n, c):
                    if n:
                        nc.vector.wait_ge(s["x_upd"], NP2 * (n - 1) + 2 * c + 2)
                    else:
                        nc.vector.wait_ge(x_in[c], 16)
                    ts = slice(4 * c, 4 * c + 4)
                    for t in range(4 * c, 4 * c + 4):
                        nc.vector.bn_stats(stats[:, t], x[:, t]).then_inc(s["ln_stats"], 1)
                    nc.vector.wait_ge(s["ln_stats"], NT * n + 4 * c + 4)
                    for t in range(4 * c, 4 * c + 4):
                        nc.vector.bn_aggr(mv[:, t], stats[:, t]).then_inc(s["ln_aggr"], 1)
                    nc.vector.wait_ge(s["ln_aggr"], NT * n + 4 * c + 4)
                    nc.vector.tensor_scalar(varep[:, ts], mv[:, ts, 1], EPS, None, ALU.add).then_inc(s["ln_vareps"], 1)
                    nc.vector.wait_ge(s["ln_vareps"], NC * n + c + 1)
                    rsqrt(rstd[:, ts], varep[:, ts], ntmp[:, 0:4])
                    for t in range(4 * c, 4 * c + 4):
                        nc.vector.tensor_scalar(xns[n][:, t], x[:, t], mv[:, t, 0:1], rstd[:, t:t + 1], ALU.subtract,
                                                ALU.mult).then_inc(s["xn_done"], 1)

                def ln_pe(n, c):
                    for t in range(4 * c, 4 * c + 4):
                        nc.tensor.wait_ge(s["xn_done"], NT * n + t + 1)
                        for k in range(KT):
                            last = nc.tensor.transpose(ps(2 * c + k)[:, (t % 4) * P:(t % 4 + 1) * P],
                                                       xns[n][:, t, k * P:(k + 1) * P], ident[:])
                            if t % 4 == 3:
                                last.then_inc(s["xT_ps"], 1)

                def ln_act(n, c):
                    for k in range(KT):
                        nc.scalar.wait_ge(s["xT_ps"], 4 * n + 2 * c + k + 1)
                        nc.scalar.copy(xnT[:, k, PAD + CH * c:PAD + CH * (c + 1)], ps(2 * c + k)).then_inc(s["xT"], 1)

                def xT_ready(eng, n, c=NC - 1):
                    eng.wait_ge(s["xT"], 4 * n + 2 * c + 2)

                def tok(t):
                    return slice(PAD + t * P, PAD + (t + 1) * P)

                def ffn_pool(f, n):
                    for c in range(NC):
                        xT_ready(nc.gpsimd, n, c)
                        for k in range(KT):
                            nc.gpsimd.tensor_scalar(xm[1][:, k, c * CH:(c + 1) * CH],
                                                    xnT[:, k, PAD - 1 + c * CH:PAD - 1 + (c + 1) * CH], mu[:, 1, 1, k:k + 1],
                                                    zcol[:], ALU.mult, ALU.add).then_inc(s["mix_r"], 1)

                def ffn_dve(f, n):
                    for c in range(NC):
                        for m in range(2):
                            for k in range(KT):
                                nc.vector.wait_ge(s[("mix_k", "mix_r")[m]], 4 * f + 2 * c + k + 1)
                                nc.vector.scalar_tensor_tensor(out=xm[m][:, k, c * CH:(c + 1) * CH],
                                                               in0=xnT[:, k, PAD + c * CH:PAD + (c + 1) * CH],
                                                               scalar=mu[:, m, 0, k:k + 1], in1=xm[m][:, k, c * CH:(c + 1) * CH],
                                                               op0=ALU.mult, op1=ALU.add).then_inc(s["mix"], 1)
                    for p in range(NP2):
                        nc.vector.wait_ge(s["th_done"], NP2 * f + p + 1)
                        nc.vector.wait_ge(s["o_ps"], NP2 * f + p + 1)
                        nc.vector.scalar_tensor_tensor(out=prod[:, p % 2].rearrange("p t c -> p (t c)"),
                                                       in0=th[:, 2 * p:2 * p + 2].rearrange("p t c -> p (t c)"), scalar=1.0, in1=ps(4 + p),
                                                       op0=ALU.add, op1=ALU.mult).then_inc(s["prod_done"], 1)
                        nc.vector.wait_ge(s["prod_done"], NP2 * f + p + 1)
                        xv = x[:, 2 * p:2 * p + 2]
                        nc.vector.scalar_tensor_tensor(out=xv, in0=prod[:, p % 2], scalar=0.25, in1=xv, op0=ALU.mult,
                                                       op1=ALU.add).then_inc(s["x_upd"], 1)
                        if p % 2:
                            ln_dve(n + 1, p // 2)

                def ffn_pe(f, n):
                    for c in range(NC):
                        ln_pe(n, c)
                        nc.tensor.wait_ge(s["mix"], 8 * f + 4 * c + 2)
                        for m in range(KT):
                            for k in range(KT):
                                last = mm(ps(4 + 2 * c + m), wk0[:, k, m * P:(m + 1) * P], xm[0][:, k, c * CH:(c + 1) * CH],
                                          start=k == 0, stop=k == KT - 1)
                            last.then_inc(s["kT_ps"], 1)
                        nc.tensor.wait_ge(s["mix"], 8 * f + 4 * c + 4)
                        for p in (2 * c, 2 * c + 1):
                            for i in range(2):
                                for k in range(KT):
                                    last = mm(ps(p)[:, i * D:(i + 1) * D], xm[1][:, k, (2 * p + i) * P:(2 * p + i + 1) * P], wr0[:, k],
                                              start=k == 0, stop=k == KT - 1)
                            last.then_inc(s["r_ps"], 1)
                    for p in range(NP2):
                        nc.tensor.wait_ge(s["kact_done"], 4 * f + 2 * (p // 2) + 2)
                        for i in range(2):
                            for k in range(KT):
                                last = mm(ps(4 + p)[:, i * D:(i + 1) * D], kact[:, k, (2 * p + i) * P:(2 * p + i + 1) * P], wv0[:, k],
                                          start=k == 0, stop=k == KT - 1)
                        last.then_inc(s["o_ps"], 1)

                def ffn_act(f, n):
                    for c in range(NC):
                        ln_act(n, c)
                        xT_ready(nc.scalar, n, c)
                        for k in range(KT):
                            nc.scalar.activation(xm[0][:, k, c * CH:(c + 1) * CH], xnT[:, k, PAD - 1 + c * CH:PAD - 1 + (c + 1) * CH],
                                                 ACT.Copy, scale=mu[:, 0, 1, k:k + 1]).then_inc(s["mix_k"], 1)
                        for m in range(KT):
                            nc.scalar.wait_ge(s["kT_ps"], 4 * f + 2 * c + m + 1)
                            nc.scalar.activation(kact[:, m, c * CH:(c + 1) * CH], ps(4 + 2 * c + m), ACT.Relu).then_inc(s["relu_done"], 1)
                        for m in range(KT):
                            v = kact[:, m, c * CH:(c + 1) * CH]
                            nc.scalar.wait_ge(s["relu_done"], 4 * f + 2 * c + m + 1)
                            nc.scalar.activation(v, v, ACT.Square).then_inc(s["kact_done"], 1)
                        for p in (2 * c, 2 * c + 1):
                            nc.scalar.wait_ge(s["r_ps"], NP2 * f + p + 1)
                            nc.scalar.activation(th[:, 2 * p:2 * p + 2].rearrange("p t c -> p (t c)"), ps(p), ACT.Tanh,
                                                 scale=0.5).then_inc(s["th_done"], 1)

                def lin_pe():
                    for c in range(NC):
                        ln_pe(1, c)
                        xT_ready(nc.tensor, 1, c)
                        for m in range(KT):
                            for k in range(KT):
                                last = mm(ps(4 + 2 * c + m), wqkv[:, k, m * P:(m + 1) * P],
                                          xnT[:, k, PAD + c * CH:PAD + (c + 1) * CH], start=k == 0, stop=k == KT - 1)
                            last.then_inc(s["q_ps"], 1)
                    for p in range(NP2):
                        if p >= 2:
                            nc.tensor.wait_ge(s["kh_done"], p - 1)
                            nc.tensor.wait_ge(s["v_done"], p - 1)
                        for i in range(2):
                            for k in range(KT):
                                last = mm(ps(2 * (p % 2) + i), xnT[:, k, tok(2 * p + i)], wqkv[:, k, D:3 * D], start=k == 0,
                                          stop=k == KT - 1)
                        last.then_inc(s["kv_ps"], 1)
                    for t in range(NT):
                        nc.tensor.wait_ge(s["kh_done"], t // 2 + 1)
                        nc.tensor.wait_ge(s["qT_done"], 2 * (t // 4) + 2)
                        for k in range(KT):
                            last = nc.tensor.transpose(ps(4 + 2 * (t // 4) + k)[:, (t % 4) * P:(t % 4 + 1) * P],
                                                       kh[:, t, k * P:(k + 1) * P], ident[:])
                            if t % 4 == 3:
                                last.then_inc(s["khT_ps"], 1)
                    nc.tensor.wait_ge(s["v_done"], NP2)

                    def scores(t):
                        nc.tensor.wait_ge(s["khT_done"], 2 * (t // 4) + 2)
                        for g in range(NG):
                            u = NG * t + g
                            nc.tensor.wait_ge(s["qbd_done"], KT * t + g // 2 + 1)
                            if u >= 2:
                                nc.tensor.wait_ge(s["sc_masked"], u - 1)
                            mm(ps(u % 2), khT[:, g // 2, t * P:(t + 1) * P],
                               qbd[:, t % 2, G * g:G * g + G], start=True, stop=True).then_inc(s["sc_ps"], 1)

                    scores(0)
                    for t in range(NT):
                        if t < NT - 1:
                            if t:
                                nc.tensor.wait_ge(s["state_done"], t)
                            for g in range(NG):
                                last = mm(ps(4)[:, g * P:(g + 1) * P], kh[:, t, (g // 2) * P:(g // 2 + 1) * P],
                                          vpad[:, t, G * g:G * g + G], start=t == 0 and g == 0, stop=t == NT - 2,
                                          skip_group_check=True)
                            last.then_inc(s["st_ps"], 1)
                        y = ps(2 + t % 2)
                        if t >= 2:
                            nc.tensor.wait_ge(s["yT_done"], t - 1)
                        for g in range(NG):
                            if t:
                                nc.tensor.wait_ge(s["state_done"], t)
                                mm(y[:, g * P:(g + 1) * P], ssb[:, (t - 1) % 2, g], qT[:, g // 2, t * P:(t + 1) * P], start=True,
                                   stop=False, skip_group_check=True)
                            nc.tensor.wait_ge(s["sc_masked"], NG * t + g + 1)
                            for j in range(G):
                                last = mm(y[HP * j:HP * (j + 1), g * P:(g + 1) * P], vpad[:, t, G * g + j],
                                          scm[:, g, j * P:(j + 1) * P], start=t == 0, stop=True, skip_group_check=True,
                                          tile_position=(0, HP * j))
                        last.then_inc(s["y_ps"], 1)
                        if t < NT - 1:
                            scores(t + 1)
                    attn_out_pe(0, yT, wo0, NG, 4, lambda t: nc.tensor.wait_ge(s["yT_done"], t + 1))

                def attn_out_pe(n, yt, w, kn, b0, ready):
                    for p in range(NP2):
                        for i in range(2):
                            ready(2 * p + i)
                            for g in range(kn):
                                last = mm(ps(b0 + p)[:, i * D:(i + 1) * D], yt[:, g, (2 * p + i) * P:(2 * p + i + 1) * P], w[:, g],
                                          start=g == 0, stop=g == kn - 1)
                        last.then_inc(s["oproj_ps"], 1)

                def attn_out_dve(n, ln, b0):
                    for p in range(NP2):
                        nc.vector.wait_ge(s["oproj_ps"], NP2 * n + p + 1)
                        xv = x[:, 2 * p:2 * p + 2]
                        nc.vector.tensor_tensor(xv, xv, ps(b0 + p).rearrange("p (t c) -> p t c", t=2), ALU.add).then_inc(s["x_upd"], 1)
                        if p % 2:
                            ln_dve(ln, p // 2)

                def lin_act():
                    for c in range(NC):
                        ln_act(1, c)
                        for m in range(KT):
                            nc.scalar.wait_ge(s["q_ps"], 2 * c + m + 1)
                            nc.scalar.copy(qT[:, m, c * CH:(c + 1) * CH], ps(4 + 2 * c + m)).then_inc(s["qT_done"], 1)
                    for p in range(NP2):
                        nc.scalar.wait_ge(s["kv_ps"], p + 1)
                        if p >= 2:
                            nc.scalar.wait_ge(s["kvar_done"], p - 1)
                        kv = ps(2 * (p % 2), 2).rearrange("p (t c) -> p t c", t=2)
                        nc.scalar.activation(ksq[:, p % 2], kv[:, :, 0:D], ACT.Square).then_inc(s["ksq_done"], 1)
                        nc.scalar.copy(vpad[:, 2 * p:2 * p + 2, :, 0:DK],
                                       kv[:, :, D:2 * D].rearrange("p t (h d) -> p t h d", h=H)).then_inc(s["v_done"], 1)
                    for c in range(NC):
                        for k in range(KT):
                            nc.scalar.wait_ge(s["khT_ps"], 2 * c + k + 1)
                            nc.scalar.copy(khT[:, k, c * CH:(c + 1) * CH], ps(4 + 2 * c + k)).then_inc(s["khT_done"], 1)
                    for t in range(NT):
                        nc.scalar.wait_ge(s["y_ps"], t + 1)
                        nc.scalar.copy(yT[:, :, t * P:(t + 1) * P], ps(2 + t % 2).rearrange("p (g c) -> p g c", g=NG)).then_inc(s["yT_done"], 1)

                def lin_pool():
                    nc.gpsimd.wait_ge(s["x_upd"], NP2)
                    for t in range(NT):
                        nc.gpsimd.wait_ge(s["qT_done"], 2 * (t // 4) + 2)
                        if t >= 2:
                            nc.gpsimd.wait_ge(s["sc_ps"], NG * (t - 1))
                        for k in range(KT):
                            nc.gpsimd.tensor_tensor(qbd[:, t % 2, 8 * k:8 * k + 8], qT[:, k, t * P:(t + 1) * P].unsqueeze(1).broadcast_to([P, 8, P]),
                                                    hmask[:].unsqueeze(2).broadcast_to([P, 8, P]), ALU.mult).then_inc(s["qbd_done"], 1)

                def lin_dve():
                    for p in range(NP2):
                        nc.vector.wait_ge(s["ksq_done"], p + 1)
                        nc.vector.reduce_sum(kvar[:, p % 2].rearrange("p t h -> p (t h)"),
                                             ksq[:, p % 2].rearrange("p t (h d) -> p (t h) d", h=H), AX).then_inc(s["kvar_done"], 1)
                        nc.vector.wait_ge(s["kvar_done"], p + 1)
                        v = kvar[:, p % 2].rearrange("p t h -> p (t h)")
                        nc.vector.tensor_scalar(v, v, DK * EPS, None, ALU.add).then_inc(s["kvar_eps"], 1)
                        nc.vector.wait_ge(s["kvar_eps"], p + 1)
                        rsqrt(krs[:, p % 2].rearrange("p t h -> p (t h)"), v, ntmp[:])
                        nc.vector.wait_ge(s["v_done"], p + 1)
                        for i in range(2):
                            last = nc.vector.scalar_tensor_tensor(
                                out=kh[:, 2 * p + i].rearrange("p (h d) -> p h d", h=H),
                                in0=ps(2 * (p % 2) + i)[:, 0:D].rearrange("p (h d) -> p h d", h=H), scalar=math.sqrt(DK),
                                in1=krs[:, p % 2, i].unsqueeze(2).broadcast_to([P, H, DK]), op0=ALU.mult, op1=ALU.mult)
                        last.then_inc(s["kh_done"], 1)
                    for t in range(NT):
                        for g in range(NG):
                            nc.vector.wait_ge(s["sc_ps"], NG * t + g + 1)
                            if t:
                                nc.vector.wait_ge(s["y_ps"], t)
                            nc.vector.tensor_tensor(scm[:, g].rearrange("p (j c) -> p j c", j=G),
                                                    ps((NG * t + g) % 2).rearrange("p (j c) -> p j c", j=G),
                                                    mask01[:].unsqueeze(1).broadcast_to([P, G, P]), ALU.mult).then_inc(s["sc_masked"], 1)
                        if t < NT - 1:
                            nc.vector.wait_ge(s["st_ps"], t + 1)
                            nc.vector.tensor_tensor(ssb[:, t % 2].rearrange("p (a b) c -> p a (b c)", a=2),
                                                    ps(4).rearrange("p (a c) -> p a c", a=2),
                                                    smask[:].rearrange("p h c -> p (h c)").unsqueeze(1).broadcast_to([P, 2, 2 * P]),
                                                    ALU.mult).then_inc(s["state_done"], 1)
                    attn_out_dve(0, 2, 4)

                def exp_pe(g, n):
                    for t in range(NT):
                        if t % 4 == 0:
                            ln_pe(n, t // 4)
                        xT_ready(nc.tensor, n, t // 4)
                        for k in range(KT):
                            last = mm(ps(4 + t // 4)[:, (t % 4) * RS:(t % 4) * RS + RW], xnT[:, k, tok(t)], wroute[:, k],
                                      start=k == 0, stop=k == KT - 1)
                        if t % 4 == 3:
                            last.then_inc(s["rt_ps"], 1)
                    for t in range(NT):
                        for k in range(KT):
                            mm(ps(t // 2)[:, (t % 2) * D:(t % 2 + 1) * D], xnT[:, k, tok(t)], wf1[:, k], start=k == 0 and t % 2 == 0,
                               stop=False, skip_group_check=True)
                    nc.tensor.wait_ge(s["rt_step"], RSTEPS * (g + 1))
                    for t in range(NT):
                        last = nc.tensor.transpose(ps(6, 2)[0:NR, t * P:(t + 1) * P], dg[:, t, 0:NR], ident[:])
                    last.then_inc(s["dgT_ps"], 1)
                    nc.tensor.wait_ge(s["dgT_done"], g + 1)
                    for t in range(NT):
                        last = mm(ps(t // 2)[:, (t % 2) * D:(t % 2 + 1) * D], dgT[0:NR, t], wup[0:NR], start=False, stop=True,
                                  skip_group_check=True)
                        if t % 2:
                            last.then_inc(s["base_ps"], 1)

                def exp_act(g, n):
                    for c in range(NC):
                        ln_act(n, c)
                    nc.scalar.wait_ge(s["rt_step"], RSTEPS * g + 1)
                    nc.scalar.activation(psq[:], projb[:], ACT.Square).then_inc(s["rt_act"], 1)
                    nc.scalar.wait_ge(s["rt_step"], RSTEPS * g + 7)
                    nc.scalar.activation(small[:, 4], small[:, 3], ACT.Exp).then_inc(s["rt_act"], 1)
                    nc.scalar.wait_ge(s["dgT_ps"], g + 1)
                    nc.scalar.copy(dgT[0:NR].rearrange("p q c -> p (q c)"), ps(6, 2)[0:NR, :]).then_inc(s["dgT_done"], 1)

                RSTEPS = 18

                def exp_dve(g, n):
                    step = [RSTEPS * g]

                    def then(ins, wait=True):
                        step[0] += 1
                        ins.then_inc(s["rt_step"], 1)
                        if wait:
                            nc.vector.wait_ge(s["rt_step"], step[0])

                    def row(i, shape=None):
                        return small[:, i].rearrange("p (t e) -> p t e", t=NT)

                    def one(i):
                        return small[:, i, 0:NT]

                    def over(v):
                        return v.unsqueeze(2).broadcast_to([P, NT, NE])

                    rt = ps(4, 2).rearrange("p (b c) -> p b c", b=2)[:, :, 0:4 * RS].rearrange("p b (t c) -> p b t c", t=4)
                    nc.vector.wait_ge(s["rt_ps"], 2 * g + 2)
                    for b in range(2):
                        last = nc.vector.tensor_tensor(projb[:, 4 * b:4 * b + 4], rt[:, b, :, 0:PROJ],
                                                       bpb[:].unsqueeze(1).broadcast_to([P, 4, PROJ]), ALU.add)
                    then(last, False)
                    for b in range(2):
                        last = nc.vector.tensor_tensor(row(0)[:, 4 * b:4 * b + 4], rt[:, b, :, PROJ + NR:RW],
                                                       bsb[:].unsqueeze(1).broadcast_to([P, 4, NE]), ALU.add)
                    then(last, False)
                    nc.vector.wait_ge(s["rt_act"], 2 * g + 1)
                    then(nc.vector.reduce_sum(one(1), psq[:], AX))
                    then(nc.vector.tensor_scalar(one(1), one(1), 1e-24, None, ALU.max))
                    rsqrt(one(11), one(1), one(12))
                    then(nc.vector.tensor_tensor(row(0), row(0), over(one(11)), ALU.mult))
                    then(nc.vector.reduce_max(one(2), row(0), AX))
                    then(nc.vector.tensor_tensor(row(3), row(0), over(one(2)), ALU.subtract))
                    then(nc.vector.tensor_scalar(row(5), row(3), 0.0, None, ALU.is_equal))
                    then(nc.vector.tensor_tensor(row(5), row(5), first[:].unsqueeze(1).broadcast_to([P, NT, NE]), ALU.mult))
                    then(nc.vector.reduce_max(one(6), row(5), AX))
                    then(nc.vector.tensor_tensor(row(7), row(5), over(one(6)), ALU.is_equal))
                    nc.vector.wait_ge(s["rt_act"], 2 * g + 2)
                    then(nc.vector.reduce_sum(one(8), row(4), AX))
                    then(nc.vector.reciprocal(one(9), one(8)))
                    then(nc.vector.tensor_tensor(row(10), row(7), over(one(9)), ALU.mult))
                    r0 = 0
                    for e, r in enumerate(RANKS):
                        for b in range(2):
                            last = nc.vector.tensor_tensor(dg[:, 4 * b:4 * b + 4, r0:r0 + r], rt[:, b, :, PROJ + r0:PROJ + r0 + r],
                                                           row(10)[:, 4 * b:4 * b + 4, e:e + 1].broadcast_to([P, 4, r]), ALU.mult)
                        then(last, False)
                        r0 += r
                    assert step[0] == RSTEPS * (g + 1)
                    for p in range(NP2):
                        nc.vector.wait_ge(s["base_ps"], NP2 * g + p + 1)
                        xv = x[:, 2 * p:2 * p + 2]
                        nc.vector.scalar_tensor_tensor(out=xv, in0=ps(p).rearrange("p (t c) -> p t c", t=2), scalar=0.5, in1=xv,
                                                       op0=ALU.mult, op1=ALU.add).then_inc(s["x_upd"], 1)
                        if g == 0 and p % 2:
                            ln_dve(n + 1, p // 2)

                ND = 6
                tunits = [(c, kb, hp) for c in range(NC) for kb in range(4 * (c + 1)) for hp in range(2)]
                NTU = len(tunits)
                sunits = [(h, qb, k0, min(P * (qb + 1), k0 + CH)) for h in range(G) for qb in range(NT)
                          for k0 in range(0, P * (qb + 1), CH)]
                NSU = len(sunits)
                PER = 3
                Y_AT = (11, 3)
                RB = 3
                MT_AT = math.ceil(NSU / PER) + 1

                EARLY = 9

                def spread(g, i):
                    at = PER * i + (EARLY if g == 0 else 0)
                    return range(min(at, NSU), min(at + PER, NSU))

                DIAG = [u for u, (c, kb, hp) in enumerate(tunits) if kb >= 4 * c]

                def width(c, kb):
                    return CH - max(0, kb - 4 * c) * P

                ring = {}
                for k in range(NSU):
                    ring["s", 0, k] = len(ring)
                ring["m", 0, 0] = len(ring)
                for k in range(EARLY):
                    ring["s", 1, k] = len(ring)
                for u in range(NTU * NG + 2):
                    g, i = divmod(u, NTU)
                    if g + 1 < NG:
                        for k in spread(g, i):
                            ring["s", g + 1, k] = len(ring)
                        if i == MT_AT:
                            ring["m", g + 1, 0] = len(ring)
                    if i == Y_AT[0]:
                        ring["y", g, 0] = len(ring)
                    if i == Y_AT[1] and g:
                        ring["y", g - 1, 1] = len(ring)
                ring["y", NG - 1, 1] = len(ring)

                def ring_bank(*unit):
                    return ps(5 + ring[unit] % RB)

                def ring_free(*unit):
                    if ring[unit] >= RB:
                        nc.tensor.wait_ge(s["ring_used"], ring[unit] - RB + 1)

                def ring_filled(*unit):
                    nc.vector.wait_ge(s["ring_full"], ring[unit] + 1)

                def sm_sync():
                    sp = nc.sync
                    sp.wait_ge(s["x_upd"], 4 * NP2)
                    sp.dma_start(ropet[:].rearrange("p a t -> p (a t)"),
                                 rope_d.rearrange("i a t -> i (a t)").unsqueeze(1).broadcast_to([DK // 2, H, 4 * T])).then_inc(s["rope_in"], 16)
                    for u in range(2 * NC):
                        c, qk = u // 2, u % 2
                        cs = slice(c * CH, (c + 1) * CH)
                        dst = (q_d, k_d)[qk]
                        sp.wait_ge(s["rope_hi"], u + 1)
                        sp.dma_start(dst[0].rearrange("o r t -> r o t")[:, :, cs], rhi[:, u % 2]).then_inc(halves_out[u % 2], 16)
                        sp.wait_ge(s["rope_lo"], u + 1)
                        sp.dma_start(dst[1].rearrange("o r t -> r o t")[:, :, cs], rlo[:, u % 2]).then_inc(halves_out[u % 2], 16)
                    for i in range(2):
                        sp.wait_ge(halves_out[i], 16 * 2 * NC)
                    for g in range(NG):
                        b = g % NST
                        if g == NST - 1:
                            sp.wait_ge(s["third_rows"], 3)
                        if g >= NST:
                            max_rows(g - NST)
                            max_rows(g - NST + 1)
                            sp.wait_ge(s["t_ps"], NTU * (g - NST + 1))
                            sp.wait_ge(max_in[b], 32 * (g // NST))
                        sp.dma_start(stq[b][MROW:MROW + 2].bitcast(F32).rearrange("p h t -> p (h t)"), zero_d).then_inc(stack_in[b], 16)

                        def rows(dram, half, n):
                            v = dram.rearrange("s o (i h) t -> (s o i) (h t)", h=H)
                            return v[DK * half:DK * (half + n), G * T * g:G * T * (g + 1)]

                        for st, r, src in ((stq[b], 0, rows(q_d, 0, 2)), (stq[b], 2, rows(q_d, 0, 2)), (stk[b], 0, rows(k_d, 0, 2)),
                                           (stk[b], 2, rows(k_d, 1, 1)), (stk[b], 3, rows(k_d, 0, 1))):
                            n = src.shape[0]
                            sp.dma_start(st[DK * r:DK * r + n].bitcast(F32).rearrange("p h t -> p (h t)"), src).then_inc(stack_in[b], 16)
                    for g in range(NG - NST + 1, NG):
                        max_rows(g)

                def max_rows(g):
                    nc.sync.wait_ge(s["ring_used"], ring["m", g, 0] + 1)
                    for i, m in enumerate((mhi, mlo)):
                        nc.sync.dma_start(stq[g % NST][MROW + i:MROW + i + 1].bitcast(F32).rearrange("o h t -> o (h t)"),
                                          m[:, g % 2].bitcast(F32)).then_inc(max_in[g % NST], 16)

                def sm_pe():
                    for c in range(NC):
                        ln_pe(4, c)
                        xT_ready(nc.tensor, 4, c)
                        for qk, w in enumerate((wq1, wk1)):
                            u = 2 * c + qk
                            if u >= 2:
                                nc.tensor.wait_ge(s["rope_ab"], 3 * (u - 1))
                            for m in range(KT):
                                for k in range(KT):
                                    last = mm(ps(4 + 2 * (u % 2) + m), w[:, k, m * P:(m + 1) * P], xnT[:, k, PAD + c * CH:PAD + (c + 1) * CH],
                                              start=k == 0, stop=k == KT - 1)
                            last.then_inc(s["qk_ps"], 1)
                    for p in range(NP2):
                        for i in range(2):
                            for k in range(KT):
                                last = mm(ps(p)[:, i * D:(i + 1) * D], xnT[:, k, tok(2 * p + i)], wv1[:, k], start=k == 0, stop=k == KT - 1)
                        last.then_inc(s["v1_ps"], 1)

                    def score(g, i):
                        h, qb, k0, k1 = sunits[i]
                        if i == 0:
                            nc.tensor.wait_ge(stack_in[g % NST], 16 * ND * (g // NST + 1))
                        ring_free("s", g, i)
                        bank = ring_bank("s", g, i)
                        diag = k1 == P * (qb + 1)
                        last = mm(bank[:, 0:k1 - k0], stq[g % NST][:, h, qb * P:(qb + 1) * P], stk[g % NST][:, h, k0:k1],
                                  start=True, stop=not diag)
                        if diag:
                            last = mm(bank[:, k1 - k0 - P:k1 - k0], identb[:], maskneg[:], start=False, stop=True)
                        last.then_inc(s["ring_full"], 1)

                    def max_transpose(g):
                        nc.tensor.wait_ge(s["mx_comb"], g + 1)
                        ring_free("m", g, 0)
                        nc.tensor.transpose(ring_bank("m", g, 0)[0:G * NT, 0:P], mxa[:, g % 2], ident[:]).then_inc(s["ring_full"], 1)

                    def tscore(g, i):
                        c, kb, hp = tunits[i]
                        u = NTU * g + i
                        if i == 0:
                            nc.tensor.wait_ge(max_in[g % NST], 32 * (g // NST + 1))
                        if u >= 2:
                            nc.tensor.wait_ge(s["exp_done"], u - 1)
                        n = width(c, kb)
                        for j in range(2):
                            last = mm(ps(2 * (u % 2) + j)[:, 0:n], stk[g % NST][:, 2 * hp + j, kb * P:(kb + 1) * P],
                                      stq[g % NST][:, 2 * hp + j, (c + 1) * CH - n:(c + 1) * CH], start=True, stop=True)
                        last.then_inc(s["t_ps"], 1)

                    def values(g, i):
                        c, kb, _ = tunits[i]
                        u = NTU * g + i
                        yu = NC * g + c
                        n = width(c, kb)
                        nc.tensor.wait_ge(s["exp_done"], u + 1)
                        if i in DIAG:
                            nc.tensor.wait_ge(s["causal_done"], len(DIAG) * g + DIAG.index(i) + 1)
                        if kb == 0 and yu >= 1:
                            nc.tensor.wait_ge(s["ypv_done"], yu)
                        for j in range(G):
                            last = mm(ps(4)[HP * j:HP * (j + 1), CH - n:CH], vpad[:, kb, G * g + j], pexp[:, (u - 1 + j // 2) % NPX, j % 2, 0:n],
                                      start=kb == 0, stop=kb == 4 * c + 3, tile_position=(0, HP * j))
                        last.then_inc(s["pv_done"], 1)

                    def y_transpose(g, c):
                        yu = NC * g + c
                        nc.tensor.wait_ge(s["ypv_done"], yu + 1)
                        ring_free("y", g, c)
                        for b in range(4):
                            last = nc.tensor.transpose(ring_bank("y", g, c)[:, b * P:(b + 1) * P], ypv[:, yu % 2, b * P:(b + 1) * P], ident[:])
                        last.then_inc(s["ring_full"], 1)

                    for i in range(NSU):
                        score(0, i)
                    max_transpose(0)
                    nc.tensor.wait_ge(s["v1_done"], NP2)
                    for k in range(EARLY):
                        score(1, k)
                    tscore(0, 0)
                    for u in range(NTU * NG + 2):
                        g, i = divmod(u, NTU)
                        if u + 1 < NTU * NG:
                            tscore(*divmod(u + 1, NTU))
                        if g + 1 < NG:
                            for k in spread(g, i)[:2]:
                                score(g + 1, k)
                        if u % 2 and u >= 3:
                            values(*divmod(u - 2, NTU))
                        if g + 1 < NG:
                            for k in spread(g, i)[2:]:
                                score(g + 1, k)
                            if i == MT_AT:
                                max_transpose(g + 1)
                        if i == Y_AT[0]:
                            y_transpose(g, 0)
                        if i == Y_AT[1] and g:
                            y_transpose(g - 1, 1)
                    y_transpose(NG - 1, 1)
                    nc.tensor.wait_ge(s["exp_done"], NTU * NG)
                    for c in range(NC):
                        nc.tensor.wait_ge(s["ring_used"], ring["y", NG - 1, c] + 1)
                        for k in range(KT):
                            for b in range(4):
                                last = nc.tensor.transpose(ps(2 + k)[:, b * P:(b + 1) * P],
                                                           ytok[:, 4 * c + b, k * P:(k + 1) * P], ident[:])
                            last.then_inc(s["yT1_ps"], 1)
                        nc.tensor.wait_ge(s["yT1_done"], 2 * c + 2)
                    attn_out_pe(1, yT1, wo1, KT, 4, lambda t: None)

                def sm_dve():
                    nc.vector.wait_ge(s["rope_in"], 16)
                    def low_half(u):
                        nc.vector.wait_ge(s["rope_hi"], u + 1)
                        if u >= 2:
                            nc.vector.wait_ge(halves_out[u % 2], 32 * (u // 2))
                        nc.vector.tensor_tensor(rlo[:, u % 2].bitcast(F32R), ra[:, u % 2], rhi[:, u % 2], ALU.subtract).then_inc(s["rope_lo"], 1)

                    for u in range(2 * NC):
                        c = u // 2
                        cs = slice(c * CH, (c + 1) * CH)
                        nc.vector.wait_ge(s["qk_ps"], u + 1)
                        if u >= 2:
                            low_half(u - 2)
                            nc.vector.wait_ge(s["rope_lo"], u - 1)
                        src = ps(4 + 2 * (u % 2), 2).rearrange("p (o c) -> p o c", o=2)
                        nc.vector.tensor_tensor(ra[:, u % 2], src, ropet[:, 0:2, cs], ALU.mult).then_inc(s["rope_ab"], 1)
                        for o in range(2):
                            nc.vector.tensor_tensor(rb[:, u % 2, o], src[:, 1 - o], ropet[:, 2 + o, cs], ALU.mult).then_inc(s["rope_ab"], 1)
                    for u in (2 * NC - 2, 2 * NC - 1):
                        low_half(u)

                    def maxima(g, i):
                        h, qb, k0, k1 = sunits[i]
                        dst = mxa[:, g % 2, NT * h + qb:NT * h + qb + 1] if k0 == 0 else mxb[:, g % 2, 4 * h + qb - 4:4 * h + qb - 3]
                        ring_filled("s", g, i)
                        nc.vector.reduce_max(dst, ring_bank("s", g, i)[:, 0:k1 - k0], AX).then_inc(s["ring_used"], 1)

                    def combine(g):
                        nc.vector.wait_ge(s["ring_used"], ring["s", g, NSU - 1] + 1)
                        late = mxa[:, g % 2].rearrange("p (h q) -> p h q", h=G)[:, :, NT // 2:NT]
                        nc.vector.tensor_tensor(late, late, mxb[:, g % 2].rearrange("p (h q) -> p h q", h=G), ALU.max).then_inc(s["mx_comb"], 1)

                    def negate(g):
                        ring_filled("m", g, 0)
                        mt = ring_bank("m", g, 0)[0:G * NT, 0:P]
                        if g >= 2:
                            nc.vector.wait_ge(max_in[(g - 2) % NST], 32 * ((g - 2) // NST + 1))
                        nc.vector.tensor_scalar(mhi[:, g % 2], mt, -1.0, None, ALU.mult).then_inc(s["m_hl"], 1)
                        nc.vector.wait_ge(s["m_hl"], g + 1)
                        nc.vector.scalar_tensor_tensor(out=mlo[:, g % 2], in0=mt, scalar=-1.0,
                                                       in1=mhi[:, g % 2].bitcast(F32), op0=ALU.mult,
                                                       op1=ALU.subtract).then_inc(s["ring_used"], 1)

                    def finish(g, c):
                        yu = NC * g + c
                        yt = ring_bank("y", g, c).rearrange("p (b j r) -> p b j r", b=4, j=G)
                        ring_filled("y", g, c)
                        nc.vector.reciprocal(yrec[:, yu % 2], yt[:, :, :, DK]).then_inc(s["y_rec"], 1)
                        nc.vector.wait_ge(s["y_rec"], yu + 1)
                        nc.vector.tensor_tensor(ytok[:, 4 * c:4 * c + 4, G * DK * g:G * DK * (g + 1)].rearrange("p b (j d) -> p b j d", j=G),
                                                yt[:, :, :, 0:DK], yrec[:, yu % 2].unsqueeze(3).broadcast_to([P, 4, G, DK]),
                                                ALU.mult).then_inc(s["ring_used"], 1)

                    for i in range(NSU):
                        maxima(0, i)
                    combine(0)
                    negate(0)
                    for k in range(EARLY):
                        maxima(1, k)
                    for g in range(NG):
                        for i in range(NTU):
                            if g + 1 < NG:
                                for k in spread(g, i):
                                    maxima(g + 1, k)
                                    if k == NSU - 1:
                                        combine(g + 1)
                                if i == MT_AT:
                                    negate(g + 1)
                            if i == Y_AT[0]:
                                finish(g, 0)
                            if i == Y_AT[1] and g:
                                finish(g - 1, 1)
                    finish(NG - 1, 1)
                    attn_out_dve(1, 5, 4)

                def sums_out(g, c):
                    nc.scalar.wait_ge(s["pv_done"], (NTU * g + (8 if c == 0 else NTU)) // 2)
                    if NC * g + c >= 2:
                        nc.scalar.wait_ge(s["ring_full"], ring["y", g - 1, c] + 1)
                    nc.scalar.copy(ypv[:, c], ps(4)).then_inc(s["ypv_done"], 1)

                def sm_act():
                    for c in range(NC):
                        ln_act(4, c)
                    for u in range(2 * NC):
                        nc.scalar.wait_ge(s["rope_r"], u + 1)
                        if u >= 2:
                            nc.scalar.wait_ge(halves_out[u % 2], 32 * (u // 2))
                        nc.scalar.copy(rhi[:, u % 2].bitcast(F32R), ra[:, u % 2]).then_inc(s["rope_hi"], 1)
                    for p in range(NP2):
                        nc.scalar.wait_ge(s["v1_ps"], p + 1)
                        nc.scalar.copy(vpad[:, 2 * p:2 * p + 2, :, 0:DK],
                                       ps(p).rearrange("p (t h d) -> p t h d", t=2, h=H)).then_inc(s["v1_done"], 1)
                    for g in range(NG):
                        for i, (c, kb, hp) in enumerate(tunits):
                            u = NTU * g + i
                            n = width(c, kb)
                            nc.scalar.wait_ge(s["t_ps"], u + 1)
                            if u >= NPX:
                                nc.scalar.wait_ge(s["pv_done"], (u - NPX) // 2 + 1)
                            nc.scalar.activation(pexp[:, u % NPX, :, 0:n], ps(2 * (u % 2), 2).rearrange("p (j c) -> p j c", j=2)[:, :, 0:n],
                                                 ACT.Exp, scale=DK ** -0.5).then_inc(s["exp_done"], 1)
                            for at, gy, cy in ((10, g, 0), (2, g - 1, 1)):
                                if i == at and gy >= 0:
                                    sums_out(gy, cy)
                    sums_out(NG - 1, 1)
                    for c in range(NC):
                        for k in range(KT):
                            nc.scalar.wait_ge(s["yT1_ps"], 2 * c + k + 1)
                            nc.scalar.copy(yT1[:, k, c * CH:(c + 1) * CH], ps(2 + k)).then_inc(s["yT1_done"], 1)

                def sm_pool():
                    for u in range(2 * NC):
                        c, qk = u // 2, u % 2
                        nc.gpsimd.wait_ge(s["rope_ab"], 3 * (u + 1))
                        nc.gpsimd.tensor_tensor(ra[:, u % 2], ra[:, u % 2], rb[:, u % 2], ALU.add).then_inc(s["rope_r"], 1)
                    nc.gpsimd.wait_ge(s["rope_lo"], 2 * NC)
                    for h in halves_out:
                        nc.gpsimd.wait_ge(h, 16 * 2 * NC)
                    for st in (stq[2], stk[2]):
                        nc.gpsimd.memset(st[MROW:P].bitcast(F32), 0.0).then_inc(s["third_rows"], 1)
                    nc.gpsimd.wait_ge(s["third_rows"], 2)
                    nc.gpsimd.memset(stk[2][MROW:MROW + 2].bitcast(F32), 1.0).then_inc(s["third_rows"], 1)
                    for g in range(NG):
                        for i in DIAG:
                            u = NTU * g + i
                            nc.gpsimd.wait_ge(s["exp_done"], u + 1)
                            v = pexp[:, u % NPX, :, 0:P]
                            nc.gpsimd.affine_select(out=v, in_=v, compare_op=ALU.is_ge, fill=0.0, base=0, pattern=[[0, 2], [1, P]],
                                                    channel_multiplier=-1).then_inc(s["causal_done"], 1)

                def chunk(dram, c):
                    return dram.rearrange("b t c -> (b t) c")[bass.ds(it * T + c * CH, CH)].rearrange("(t p) c -> p t c", p=P)

                @block.sync
                def _(sp):
                    for c in range(NC):
                        sp.dma_start(x[:, 4 * c:4 * c + 4], chunk(a["L0_attn_x"], c)).then_inc(x_in[c], 16)
                    sm_sync()
                    for c in range(NC):
                        sp.wait_ge(s["x_upd"], 5 * NP2 + 2 * c + 2)
                        sp.dma_start(chunk(out, c), x[:, 4 * c:4 * c + 4]).then_inc(s["x_out"], 16)
                    sp.wait_ge(s["x_out"], 16 * NC)

                @block.gpsimd
                def _(pool):
                    ffn_pool(0, 0)
                    lin_pool()
                    ffn_pool(1, 2)
                    sm_pool()

                @block.scalar
                def _(act):
                    ffn_act(0, 0)
                    lin_act()
                    ffn_act(1, 2)
                    exp_act(0, 3)
                    sm_act()
                    exp_act(1, 5)

                @block.vector
                def _(dve):
                    for c in range(NC):
                        ln_dve(0, c)
                    ffn_dve(0, 0)
                    lin_dve()
                    ffn_dve(1, 2)
                    exp_dve(0, 3)
                    sm_dve()
                    exp_dve(1, 5)

                @block.tensor
                def _(pe):
                    ffn_pe(0, 0)
                    lin_pe()
                    ffn_pe(1, 2)
                    exp_pe(0, 3)
                    sm_pe()
                    exp_pe(1, 5)

            for v in s.values():
                nc.gpsimd.sem_clear(v)
            nc.all_engine_barrier()


_INS = (["L0_attn_x", "L0_attn_W_qkv", "L0_attn_W_o", "L0_ffn_W_r", "L0_ffn_W_k", "L0_ffn_W_v", "L0_ffn_mu_r",
         "L0_ffn_mu_k", "L1_attn_Wq", "L1_attn_Wk", "L1_attn_Wv", "L1_attn_Wo", "L1_ffn_W", "L1_ffn_Wp", "L1_ffn_bp",
         "L1_ffn_sim", "L1_ffn_temp"] + [f"L1_ffn_W{k}{e}" for e in range(NE) for k in "du"])


def kernel(**inputs):
    import concourse.bacc as _bacc
    from concourse.bass_utils import run_bass_kernel_spmd as _run

    nc = _bacc.Bacc("TRN2", target_bir_lowering=False, num_devices=1)
    arrays, aps = {}, {}
    for name in _INS:
        arr = np.ascontiguousarray(inputs[name])
        arrays[f"in_{name}"] = arr
        aps[name] = nc.dram_tensor(f"in_{name}", arr.shape, mybir.dt.from_np(arr.dtype), kind="ExternalInput").ap()
    out = nc.dram_tensor("out_0", (B, T, D), F32, kind="ExternalOutput").ap()
    macaron(nc, aps, out)
    r = _run(nc, [arrays], core_ids=[0])
    return r.results[0]["out_0"]
```
